# Optimizing a Trainium2 kernel written in Bass

```python
import numpy as np
import jax
import jax.numpy as jnp

def _softmax(x, axis=-1):
    return jax.nn.softmax(x, axis=axis)
def _gelu(x):
    return jax.nn.gelu(x, approximate=True)
def _silu(x):
    return jax.nn.silu(x)
def _sigmoid(x):
    return jax.nn.sigmoid(x)
def _layernorm(x, axis=-1, eps=1e-5):
    m = jnp.mean(x, axis=axis, keepdims=True)
    v = jnp.var(x, axis=axis, keepdims=True)
    return (x - m) / jnp.sqrt(v + eps)
def _scatter_add(tgt, idx, src, axis=0):
    return tgt.at[idx].add(src)
def _segment_sum(src, seg, n):
    return jax.ops.segment_sum(src, seg, n)

kernel_name = 'mk_conv_preact_d1_conv_nchw256_336103'

def setup_inputs(seed: int = 0):
    np.random.seed(seed)
    _w = jnp.asarray
    def _rec_inputs():
        import jax
        import jax.numpy as jnp
        _gk = jax.random.key(seed)
        x = -0.0002091 + 1 * jax.random.normal(jax.random.fold_in(_gk, 1), (32, 256, 56, 56), jnp.float32)
        return x
    x = _rec_inputs()
    def _L0_conv_setup():
        import jax, jax.numpy as jnp
        import numpy as np
        WS = 7
        HEADS = 4
        DH = 64
        SCALE = DH ** (-0.5)

        def _forward(x, qk_w, v_w):
            B, C, H, W = x.shape
            pad_b = (WS - H % WS) % WS
            pad_r = (WS - W % WS) % WS
            x = jnp.pad(x, ((0, 0), (0, 0), (0, pad_b), (0, pad_r)))
            Hp, Wp = (H + pad_b, W + pad_r)
            n1, n2 = (Hp // WS, Wp // WS)
            qk = jnp.einsum('bchw,oc->bohw', x, qk_w)
            v = jax.nn.relu(jnp.einsum('bchw,oc->bohw', x, v_w))

            def part_r(t):
                b, c = t.shape[:2]
                return t.reshape(b, c, WS, n1, WS, n2).transpose(0, 3, 5, 1, 2, 4).reshape(b * n1 * n2, c, WS, WS)

            def merge_r(t, b):
                c = t.shape[1]
                return t.reshape(b, n1, n2, c, WS, WS).transpose(0, 3, 4, 1, 5, 2).reshape(b, c, Hp, Wp)

            def part_c(t):
                b, c = t.shape[:2]
                return t.reshape(b, c, n1, WS, n2, WS).transpose(0, 2, 4, 1, 3, 5).reshape(b * n1 * n2, c, WS, WS)

            def merge_c(t, b):
                c = t.shape[1]
                return t.reshape(b, n1, n2, c, WS, WS).transpose(0, 3, 1, 4, 2, 5).reshape(b, c, Hp, Wp)

            def win_attn(qk_win, v_win):
                bw = qk_win.shape[0]
                N = WS * WS
                qkr = qk_win.reshape(bw, 2, HEADS, DH, N)
                q = qkr[:, 0].transpose(0, 1, 3, 2)
                k = qkr[:, 1].transpose(0, 1, 3, 2)
                dhv = v_win.shape[1] // HEADS
                vv = v_win.reshape(bw, HEADS, dhv, N).transpose(0, 1, 3, 2)
                attn = jax.nn.softmax(jnp.einsum('bhnd,bhmd->bhnm', q, k) * SCALE, axis=-1)
                o = jnp.einsum('bhnm,bhmd->bhnd', attn, vv)
                return o.transpose(0, 1, 3, 2).reshape(bw, HEADS * dhv, WS, WS)
            o_remote = merge_r(win_attn(part_r(qk), part_r(v)), B)
            o_close = merge_c(win_attn(part_c(qk), part_c(v)), B)
            out = o_remote + o_close
            return out[:, :, :H, :W]
        key = jax.random.key(seed)
        k1, k2, k3 = jax.random.split(key, 3)
        x = jax.random.normal(k1, (32, 256, 56, 56), dtype=jnp.float32)
        qk_w = jax.random.normal(k2, (512, 256), dtype=jnp.float32) * 0.02
        v_w = jax.random.normal(k3, (256, 256), dtype=jnp.float32) * 0.02
        return {'x': x, 'qk_w': qk_w, 'v_w': v_w}
    _L0_conv_all = _L0_conv_setup()
    _L0_conv_in = {k: v for k, v in _L0_conv_all.items() if k in ('qk_w', 'v_w', )}
    del _L0_conv_all

    return {
        "x": x,
        "L0_conv_qk_w": _L0_conv_in["qk_w"],
        "L0_conv_v_w": _L0_conv_in["v_w"],
    }

def reference(x, L0_conv_qk_w, L0_conv_v_w):
    import jax
    import jax.numpy as jnp
    def _L0_conv_ref(x, qk_w, v_w):
        import jax, jax.numpy as jnp
        import numpy as np
        WS = 7
        HEADS = 4
        DH = 64
        SCALE = DH ** (-0.5)

        def _forward(x, qk_w, v_w):
            B, C, H, W = x.shape
            pad_b = (WS - H % WS) % WS
            pad_r = (WS - W % WS) % WS
            x = jnp.pad(x, ((0, 0), (0, 0), (0, pad_b), (0, pad_r)))
            Hp, Wp = (H + pad_b, W + pad_r)
            n1, n2 = (Hp // WS, Wp // WS)
            qk = jnp.einsum('bchw,oc->bohw', x, qk_w)
            v = jax.nn.relu(jnp.einsum('bchw,oc->bohw', x, v_w))

            def part_r(t):
                b, c = t.shape[:2]
                return t.reshape(b, c, WS, n1, WS, n2).transpose(0, 3, 5, 1, 2, 4).reshape(b * n1 * n2, c, WS, WS)

            def merge_r(t, b):
                c = t.shape[1]
                return t.reshape(b, n1, n2, c, WS, WS).transpose(0, 3, 4, 1, 5, 2).reshape(b, c, Hp, Wp)

            def part_c(t):
                b, c = t.shape[:2]
                return t.reshape(b, c, n1, WS, n2, WS).transpose(0, 2, 4, 1, 3, 5).reshape(b * n1 * n2, c, WS, WS)

            def merge_c(t, b):
                c = t.shape[1]
                return t.reshape(b, n1, n2, c, WS, WS).transpose(0, 3, 1, 4, 2, 5).reshape(b, c, Hp, Wp)

            def win_attn(qk_win, v_win):
                bw = qk_win.shape[0]
                N = WS * WS
                qkr = qk_win.reshape(bw, 2, HEADS, DH, N)
                q = qkr[:, 0].transpose(0, 1, 3, 2)
                k = qkr[:, 1].transpose(0, 1, 3, 2)
                dhv = v_win.shape[1] // HEADS
                vv = v_win.reshape(bw, HEADS, dhv, N).transpose(0, 1, 3, 2)
                attn = jax.nn.softmax(jnp.einsum('bhnd,bhmd->bhnm', q, k) * SCALE, axis=-1)
                o = jnp.einsum('bhnm,bhmd->bhnd', attn, vv)
                return o.transpose(0, 1, 3, 2).reshape(bw, HEADS * dhv, WS, WS)
            o_remote = merge_r(win_attn(part_r(qk), part_r(v)), B)
            o_close = merge_c(win_attn(part_c(qk), part_c(v)), B)
            out = o_remote + o_close
            return out[:, :, :H, :W]
        return _forward(x, qk_w, v_w)

    def _gn(v, G=32, eps=1e-5):
        B_, C_, H_, W_ = v.shape
        g = v.reshape(B_, G, C_ // G, H_, W_)
        m = jnp.mean(g, axis=(2, 3, 4), keepdims=True)
        s = jnp.var(g, axis=(2, 3, 4), keepdims=True)
        return ((g - m) / jnp.sqrt(s + eps)).reshape(v.shape)

    def _ln_c(v, eps=1e-6):
        m = jnp.mean(v, axis=1, keepdims=True)
        s = jnp.var(v, axis=1, keepdims=True)
        return (v - m) / jnp.sqrt(s + eps)

    def _ln_t(v, eps=1e-5):
        m = jnp.mean(v, axis=-1, keepdims=True)
        s = jnp.var(v, axis=-1, keepdims=True)
        return (v - m) / jnp.sqrt(s + eps)

    def _to_tokens(v):
        B_, C_, H_, W_ = v.shape
        return v.reshape(B_, C_, H_ * W_).transpose(0, 2, 1)
    def _from_tokens(t, like):
        B_, C_, H_, W_ = like.shape
        return t.transpose(0, 2, 1).reshape(B_, C_, H_, W_)

    x = x + _L0_conv_ref(_gn(x), L0_conv_qk_w, L0_conv_v_w)
    return x


_drawn_inputs = setup_inputs


def setup_inputs(seed=0):
    import zlib

    import numpy as np

    out = dict(_drawn_inputs(seed))
    spreads = {}
    factors = {'L0_conv_qk_w': 8.0}
    for name, (base, spread) in spreads.items():
        noise = np.random.default_rng([zlib.crc32(name.encode()), seed]).standard_normal(out[name].shape)
        drawn = base * np.exp(spread * noise) if base else spread * noise
        out[name] = jnp.asarray(drawn.astype(out[name].dtype))
    for name, factor in factors.items():
        out[name] = (out[name] * factor).astype(out[name].dtype)
    return out
```

```python
import concourse.bass as bass
from concourse import mybir
from contextlib import ExitStack

F32 = mybir.dt.float32
F16 = mybir.dt.float16
ALU = mybir.AluOpType
ACT = mybir.ActivationFunctionType
AX = mybir.AxisListType.X

WS = 7
SIDE = 56
NW = SIDE // WS
PIX = SIDE * SIDE
TOK = WS * WS
SLOT = 64
P = 128
HEADS, DH = 4, 64
TILES = 2
GROUP = NW * TOK
STEPS = 32
ZEROS = 11
LAG_SUM, LAG_PARTS, LAG_TURN, LAG_V, LAG_MIX = 1, 2, 3, 3, 4
LEAD_Q = 2
AHEAD = 8
CH = 448
NCH = PIX // CH
W_TOP = 4.0
GN_EPS = 1e-5
SCALE = DH ** -0.5


def view(a, offset, dims):
    return bass.AP(a.tensor, a.offset + offset, [list(a.ap[0]), *[list(d) for d in dims]])


def window_attention(nc, x, qk_wt, v_wt, sel, grp, out):
    images = x.shape[0]
    x_d = x.rearrange("b (t p) h w -> b t p (h w)", p=P)
    out_d = out.rearrange("b (t p) h w -> b t p (h w)", p=P)

    ctx = ExitStack()
    with ctx:
        def sb(name, shape, dt):
            return ctx.enter_context(nc.sbuf_tensor(name, shape, dt))

        def pb(name, shape, dt=F32):
            return ctx.enter_context(nc.psum_tensor(name, shape, dt))

        def sem(name):
            return ctx.enter_context(nc.semaphore(name))

        img = sb("img", [P, 2, TILES, PIX], F32)
        xn_hi = sb("xn_hi", [P, 2, TILES, NW * NW * SLOT], F16)
        xn_lo = sb("xn_lo", [P, 2, TILES, NW * NW * SLOT], F16)
        q_hi = sb("q_hi", [P, 2, NW, P], F16)
        q_lo = sb("q_lo", [P, 2, NW, P], F16)
        k_hi = sb("k_hi", [P, 2, PIX], F16)
        k_lo = sb("k_lo", [P, 2, PIX], F16)
        w_f = sb("w_f", [P, TILES, 768], F32)
        w_hi = sb("w_hi", [P, TILES, 768], F16)
        w_lo = sb("w_lo", [P, TILES, 768], F16)
        select = sb("select", [P, TOK], F16)
        group_mean = sb("group_mean", [P, P], F32)
        smax = sb("smax", [P, 2, NW], F32)
        shifted = sb("shifted", [P, 2, GROUP], F32)
        exps = sb("exps", [P, 2, GROUP], F32)
        sums = sb("sums", [P, 2, NW], F32)
        rsum = sb("rsum", [P, 2, NW], F32)
        probs = sb("probs", [P, 2, GROUP], F32)
        p_hi = sb("p_hi", [P, 2, NW, P], F16)
        p_lo = sb("p_lo", [P, 2, NW, P], F16)
        pt = sb("pt", [P, 2, 2, GROUP], F16)
        v_hi = sb("v_hi", [P, 2, NW, P], F16)
        v_lo = sb("v_lo", [P, 2, NW, P], F16)
        o_sb = sb("o_sb", [P, 2, GROUP], F32)
        bn = sb("bn", [P, TILES, NCH, 6], F32)
        mv = sb("mv", [P, 2, TILES], F32)
        dev = sb("dev", [P, 3, TILES], F32)
        gstat = sb("gstat", [P, 2, TILES], F32)
        norm = sb("norm", [P, 2, TILES], F32)
        xt = sb("xt", [P, 2, GROUP], F32)
        ext = sb("ext", [P, 8], F32)
        ext_all = sb("ext_all", [P, 8], F32)
        amax = sb("amax", [P, 2], F32)
        inv_w = sb("inv_w", [P, 2], F32)
        rec_w = sb("rec_w", [P, 2], F32)
        mul_w = sb("mul_w", [P, 2], F32)
        sq_w = sb("sq_w", [P, 1], F32)
        exp_scale = sb("exp_scale", [P, 1], F32)
        v_scale = inv_w[:, 1:2]
        half = sb("half", [P, TILES], F32)

        ps_s = pb("ps_s", [P, 512])
        ps_q = pb("ps_q", [P, 512])
        ps_k = pb("ps_k", [P, 512])
        ps_v = [pb(f"ps_v{i}", [P, 512]) for i in range(2)]
        ps_t = pb("ps_t", [P, 2, 512])
        ps_o = pb("ps_o", [P, 512])
        ps_g = ps_k[:, 448:452]

        s_scores, s_max, s_shift, s_exp, s_sum, s_rsum, s_norm = map(
            sem, ("s_scores", "s_max", "s_shift", "s_exp", "s_sum", "s_rsum", "s_norm"))
        s_phi, s_plo, s_turn, s_pt, s_v, s_vhi, s_vlo, s_mix, s_osb, s_add = map(
            sem, ("s_phi", "s_plo", "s_turn", "s_pt", "s_v", "s_vhi", "s_vlo", "s_mix", "s_osb", "s_add"))
        s_q, s_k, s_qhi, s_qlo, s_khi, s_klo = map(sem, ("s_q", "s_k", "s_qhi", "s_qlo", "s_khi", "s_klo"))
        s_bn, s_mv, s_mean, s_dev1, s_dev2, s_dev, s_var, s_gstat, s_rstd, s_nmean = map(
            sem, ("s_bn", "s_mv", "s_mean", "s_dev1", "s_dev2", "s_dev", "s_var", "s_gstat", "s_rstd", "s_nmean"))
        s_xt, s_xhi, s_xlo = map(sem, ("s_xt", "s_xhi", "s_xlo"))
        s_load = [sem(f"s_load{t}") for t in range(TILES)]
        s_store = [sem(f"s_store{t}") for t in range(TILES)]
        s_const, s_zero, s_zimg, s_half, s_ext, s_all, s_w, s_wprep = map(
            sem, ("s_const", "s_zero", "s_zimg", "s_half", "s_ext", "s_all", "s_w", "s_wprep"))

        block = ctx.enter_context(nc.Block())

        class At:

            def __init__(self, it):
                self.it = it

            def step(self, g):
                return self.it * (2 * STEPS) + (AHEAD + g + 1)

            def keys(self, g):
                return self.it * 32 + (16 * (g // STEPS) + g % STEPS + 1)

            def image(self, m, per=1):
                return self.it * (2 * per) + (m + 1) * per

            def chunk(self, m, n):
                return self.it * 64 + (32 * m + n + 1)

        def place(g):
            s = g % STEPS
            return (g // STEPS) % 2, s // 16, (s // 2) % 8, s % 2

        def live(g, last):
            return last is None or g < last

        def windows(a, dilated, r):
            if dilated:
                return view(a, SIDE * r, [[1, NW], [NW * SIDE, WS], [NW, WS]])
            return view(a, WS * SIDE * r, [[WS, NW], [SIDE, WS], [1, WS]])

        def tokens(a, dilated, r, w):
            if dilated:
                return view(a, SIDE * r + w, [[NW * SIDE, WS], [NW, WS]])
            return view(a, WS * SIDE * r + WS * w, [[SIDE, WS], [1, WS]])

        def slotted(a, first=0, pitch=SLOT):
            return view(a, first, [[pitch, NW], [1, TOK]])

        def by_window(a):
            return a.rearrange("p (w t) -> p w t", t=TOK)

        def by_row(a):
            return a.rearrange("p (w a b) -> p w a b", w=NW, b=WS)

        STATS = {9: [(0, 0), (0, 1), (0, 2)], 10: [(0, 3), (0, 4)], 11: [(0, 5), (0, 6)],
                 12: [(1, 0), (1, 1), (1, 2)], 13: [(1, 3), (1, 4)], 14: [(1, 5), (1, 6)]}
        AGGREGATE, MEAN, VARIANCE, NORMAL = 15, 16, 17, 17
        ORDER = []
        for n in range(16):
            ORDER.append((18 + n // 2 if n < 6 else 15 + n, 0, n // 2, n % 2))
            ORDER.append((21 + n, 1, n // 2, n % 2))
        ORDER.sort()
        BEFORE = sum(step < STEPS for step, *_ in ORDER)
        CHUNK_OF = {(kind, r, t): n for n, (_, kind, r, t) in enumerate(ORDER)}

        def chunks(g):
            s = g % STEPS
            return [(g // STEPS + (step < STEPS), n, kind, r, t)
                    for n, (step, kind, r, t) in enumerate(ORDER) if step % STEPS == s]

        @block.sync
        def _(sp):
            def load(i, t, par):
                sp.dma_start(img[:, par, t, :], x_d[i, t]).then_inc(s_load[t], 16)

            def store(i, t, par):
                sp.dma_start(out_d[i, t], img[:, par, t, :]).then_inc(s_store[t], 16)

            for t in range(TILES):
                load(0, t, 0)
            sp.wait_ge(s_zimg, 1)
            sp.wait_ge(s_add, AHEAD)
            for t in range(TILES):
                load(1, t, 1)

            def image(at, m, nxt):
                sp.wait_ge(s_add, at.step(m * STEPS + STEPS - 1))
                for t in range(TILES):
                    store(at.it * 2 + m, t, m)
                if nxt is not None:
                    for t in range(TILES):
                        sp.wait_ge(s_store[t], at.it * 32 + 16 * (m + 1))
                        load(nxt, t, m)

            with sp.Fori(0, images // 2 - 1) as it:
                for m in range(2):
                    image(At(it), m, it * 2 + (m + 2))
            image(At(images // 2 - 1), 0, images - 1)
            image(At(images // 2 - 1), 1, None)
            for t in range(TILES):
                sp.wait_ge(s_store[t], 16 * images)

        @block.tensor
        def _(pe):
            mm = nc.tensor.matmul

            def three(o, stat, mov, first, last):
                mm(o, stat[0], mov[0], start=first, stop=False)
                mm(o, stat[0], mov[1], start=False, stop=False)
                return mm(o, stat[1], mov[0], start=False, stop=last)

            def project(bank, dil, r, hp, col):
                for c in range(TILES):
                    w = slice(col + P * hp, col + P * hp + P)
                    mov = [slotted(a[:, dil, c, :], r * NW * SLOT) for a in (xn_hi, xn_lo)]
                    last = three(bank[:, 0:GROUP], (w_hi[:, c, w], w_lo[:, c, w]), mov, c == 0, c == TILES - 1)
                return last

            def project_q(at, g):
                m, dil, r, hp = place(g)
                pe.wait_ge(s_xlo, at.chunk(g // STEPS, CHUNK_OF[dil, r, 1]))
                pe.wait_ge(s_qlo, at.step(g - 1))
                project(ps_q, dil, r, hp, 0).then_inc(s_q, 1)

            def project_k(at, g, wait=True):
                m, dil, r, hp = place(g)
                if wait:
                    pe.wait_ge(s_klo, at.keys(g) - 1)
                project(ps_k, dil, r, hp, 256).then_inc(s_k, 1)

            def mean(at, m, first=False):
                pe.wait_ge(s_mv, at.image(m))
                if not first:
                    pe.wait_ge(s_klo, at.keys(STEPS * (m - 1) + 15))
                mm(ps_g[:, 0:2], group_mean[:], mv[:, 0, :], start=True, stop=True).then_inc(s_mean, 1)

            def variance(at, m):
                pe.wait_ge(s_dev, at.image(m))
                mm(ps_g[:, 2:4], group_mean[:], dev[:, 2, :], start=True, stop=True).then_inc(s_var, 1)

            def scores(at, g):
                m, dil, r, hp = place(g)
                pe.wait_ge(s_qlo, at.step(g))
                if not dil:
                    pe.wait_ge(s_klo, at.keys(g))
                pe.wait_ge(s_shift, at.step(g - 1))
                for w in range(NW):
                    f = three(ps_s[:, w * TOK:w * TOK + TOK], (q_hi[:, g % 2, w, :], q_lo[:, g % 2, w, :]),
                              [tokens(a[:, hp, :], dil, r, w) for a in (k_hi, k_lo)], True, True)
                f.then_inc(s_scores, 1)

            def turn(at, g):
                pe.wait_ge(s_plo, at.step(g))
                pe.wait_ge(s_pt, at.step(g - 1))
                for k, part in enumerate((p_hi, p_lo)):
                    for w in range(NW):
                        f = mm(ps_t[:, k, w * TOK:w * TOK + TOK], part[:, g % 2, w, :], select[:],
                               start=True, stop=True)
                f.then_inc(s_turn, 1)

            def values(at, g):
                m, dil, r, hp = place(g)
                pe.wait_ge(s_vlo, at.step(g - 2))
                cols = slice(512 + P * hp, 512 + P * hp + P)
                for w in range(0, NW, 2):
                    for c in range(TILES):
                        at_w = slice((r * NW + w) * SLOT, (r * NW + w + 2) * SLOT)
                        f = three(ps_v[g % 2][:, w * DH:w * DH + P], [a[:, dil, c, at_w] for a in (xn_hi, xn_lo)],
                                  (w_hi[:, c, cols], w_lo[:, c, cols]), c == 0, c == TILES - 1)
                f.then_inc(s_v, 1)

            def mix(at, g):
                pe.wait_ge(s_osb, at.step(g - 1))
                pe.wait_ge(s_pt, at.step(g))
                pe.wait_ge(s_vlo, at.step(g))
                for w in range(NW):
                    t = slice(w * TOK, w * TOK + TOK)
                    f = three(ps_o[:, t], (v_hi[:, g % 2, w, :], v_lo[:, g % 2, w, :]),
                              (pt[:, g % 2, 0, t], pt[:, g % 2, 1, t]), True, True)
                f.then_inc(s_mix, 1)

            def step(at, g, last=None):
                if live(g, last):
                    scores(at, g)
                    if g % STEPS == MEAN:
                        mean(at, g // STEPS + 1)
                    if g % STEPS == VARIANCE:
                        variance(at, g // STEPS + 1)
                if live(g - LAG_TURN, last):
                    turn(at, g - LAG_TURN)
                if live(g, last):
                    project_q(at, g + LEAD_Q)
                if live(g - LAG_V, last):
                    values(at, g - LAG_V)
                if live(g, last) and not place(g + LEAD_Q)[1]:
                    project_k(at, g + LEAD_Q)
                mix(at, g - LAG_MIX)

            zero = At(0)
            pe.wait_ge(s_const, 32)
            mean(zero, 0, True)
            variance(zero, 0)
            pe.wait_ge(s_wprep, 3)
            pe.wait_ge(s_zero, ZEROS)
            for g in range(LEAD_Q):
                project_q(zero, g)
                project_k(zero, g, g > 0)
            pe.wait_ge(s_xlo, BEFORE)
            with pe.Fori(0, images // 2) as it:
                for g in range(2 * STEPS):
                    step(At(it), g)
            for g in range(2 * STEPS, 2 * STEPS + LAG_MIX):
                step(At(images // 2 - 1), g, 2 * STEPS)

        @block.scalar
        def _(act):
            def copy(o, i):
                return nc.scalar.activation(o, i, ACT.Copy)

            def q_part(at, g):
                act.wait_ge(s_q, at.step(g))
                for h in range(2):
                    o = slice(64 * h, 64 * h + 64)
                    f = copy(slotted(q_hi[o, g % 2, 0, :], 64 * h, P), by_window(ps_q[o, 0:GROUP]))
                f.then_inc(s_qhi, 1)

            def k_part(at, g):
                m, dil, r, hp = place(g)
                act.wait_ge(s_k, at.keys(g))
                copy(windows(k_hi[:, hp, :], dil, r), by_row(ps_k[:, 0:GROUP])).then_inc(s_khi, 1)

            def x_part(at, m, n, kind, r, t, first=False):
                act.wait_ge(s_xt, at.chunk(m, n))
                if not first:
                    act.wait_ge(s_v, at.step((m - 1) * STEPS + kind * 16 + 2 * r + 1))
                copy(slotted(xn_hi[:, kind, t, :], r * NW * SLOT), by_window(xt[:, n % 2, :])).then_inc(s_xhi, 1)

            def p_part(at, g):
                act.wait_ge(s_norm, at.step(g))
                for h in range(2):
                    o = slice(64 * h, 64 * h + 64)
                    f = copy(slotted(p_hi[o, g % 2, 0, :], 64 * h, P), by_window(probs[o, g % 2, :]))
                f.then_inc(s_phi, 1)

            def turned(at, g):
                act.wait_ge(s_turn, at.step(g))
                act.wait_ge(s_mix, at.step(g - 2))
                copy(pt[:, g % 2, :, :], ps_t[:, :, 0:GROUP]).then_inc(s_pt, 1)

            def exp(at, g):
                act.wait_ge(s_shift, at.step(g))
                act.wait_ge(s_norm, at.step(g - 2))
                nc.scalar.activation(exps[:, g % 2, :], shifted[:, g % 2, :], ACT.Exp,
                                     scale=exp_scale[:, 0:1]).then_inc(s_exp, 1)

            def mixed(at, g):
                act.wait_ge(s_mix, at.step(g))
                act.wait_ge(s_add, at.step(g - 2))
                nc.scalar.activation(o_sb[:, g % 2, :], ps_o[:, 0:GROUP], ACT.Copy,
                                     scale=v_scale).then_inc(s_osb, 1)

            def v_part(at, g):
                act.wait_ge(s_v, at.step(g))
                for odd in range(2):
                    for h in range(2):
                        src = ps_v[g % 2][64 * odd:64 * odd + 64, :].rearrange("p (j n) -> p j n", n=P)
                        f = nc.scalar.activation(v_hi[64 * h:64 * h + 64, g % 2, odd::2, DH * h:DH * h + DH],
                                                 src[:, :, DH * h:DH * h + DH], ACT.Relu)
                f.then_inc(s_vhi, 1)

            def step(at, g, last=None):
                if live(g - LAG_PARTS, last):
                    p_part(at, g - LAG_PARTS)
                if live(g - LAG_TURN, last):
                    turned(at, g - LAG_TURN)
                if live(g, last):
                    exp(at, g)
                mixed(at, g - LAG_MIX)
                if live(g - LAG_V, last):
                    v_part(at, g - LAG_V)
                if live(g, last):
                    q_part(at, g + LEAD_Q)
                    if not place(g + LEAD_Q)[1]:
                        k_part(at, g + LEAD_Q)
                    for chunk in chunks(g):
                        x_part(at, *chunk)

            act.dma_start(w_f[:, :, 0:512], qk_wt.rearrange("(t p) n -> p t n", p=P)).then_inc(s_w, 16)
            act.dma_start(w_f[:, :, 512:768], v_wt.rearrange("(t p) n -> p t n", p=P)).then_inc(s_w, 16)
            act.dma_start(select[:], sel).then_inc(s_const, 16)
            act.dma_start(group_mean[:], grp).then_inc(s_const, 16)
            zero = At(0)
            act.wait_ge(s_zero, ZEROS)
            for n, (step_, kind, r, t) in enumerate(ORDER):
                if step_ < STEPS:
                    x_part(zero, 0, n, kind, r, t, True)
            for g in range(LEAD_Q):
                q_part(zero, g)
                k_part(zero, g)
            act.wait_ge(s_wprep, 3)
            with act.Fori(0, images // 2) as it:
                for g in range(2 * STEPS):
                    step(At(it), g)
            for g in range(2 * STEPS, 2 * STEPS + LAG_MIX):
                step(At(images // 2 - 1), g, 2 * STEPS)

        @block.vector
        def _(dve):
            V = nc.vector

            def q_part(at, g):
                dve.wait_ge(s_qhi, at.step(g))
                for h in range(2):
                    o = slice(64 * h, 64 * h + 64)
                    f = V.tensor_tensor(slotted(q_lo[o, g % 2, 0, :], 64 * h, P), by_window(ps_q[o, 0:GROUP]),
                                        slotted(q_hi[o, g % 2, 0, :], 64 * h, P), ALU.subtract)
                f.then_inc(s_qlo, 1)

            def k_part(at, g):
                m, dil, r, hp = place(g)
                dve.wait_ge(s_khi, at.keys(g))
                V.tensor_tensor(windows(k_lo[:, hp, :], dil, r), by_row(ps_k[:, 0:GROUP]),
                                windows(k_hi[:, hp, :], dil, r), ALU.subtract).then_inc(s_klo, 1)

            def stats(at, m, t, c):
                if c == 0:
                    dve.wait_ge(s_load[t], at.image(m, 16))
                V.bn_stats(bn[:, t, c, :], img[:, m % 2, t, c * CH:c * CH + CH]).then_inc(s_bn, 1)

            def aggregate(at, m):
                for t in range(TILES):
                    f = V.bn_aggr(mv[:, :, t], bn[:, t, :, :])
                f.then_inc(s_mv, 1)

            def deviation(at, m):
                dve.wait_ge(s_mean, at.image(m))
                V.tensor_tensor(dev[:, 0, :], ps_g[:, 0:2], mv[:, 0, :], ALU.subtract)
                V.tensor_copy(gstat[:, 0, :], ps_g[:, 0:2]).then_inc(s_dev1, 1)
                dve.wait_ge(s_dev1, at.image(m))
                V.tensor_tensor(dev[:, 1, :], dev[:, 0, :], dev[:, 0, :], ALU.mult).then_inc(s_dev2, 1)
                dve.wait_ge(s_dev2, at.image(m))
                V.tensor_tensor(dev[:, 2, :], dev[:, 1, :], mv[:, 1, :], ALU.add).then_inc(s_dev, 1)

            def group_variance(at, m):
                dve.wait_ge(s_var, at.image(m))
                V.tensor_scalar(gstat[:, 1, :], ps_g[:, 2:4], GN_EPS, None, ALU.add).then_inc(s_gstat, 1)

            def shift(at, g):
                s3 = by_window(ps_s[:, 0:GROUP])
                dve.wait_ge(s_scores, at.step(g))
                V.tensor_reduce(smax[:, g % 2, :], s3, axis=AX, op=ALU.max).then_inc(s_max, 1)
                dve.wait_ge(s_max, at.step(g))
                V.tensor_tensor(by_window(shifted[:, g % 2, :]), s3,
                                smax[:, g % 2, :].unsqueeze(2).to_broadcast([P, NW, TOK]),
                                ALU.subtract).then_inc(s_shift, 1)

            def total(at, g):
                dve.wait_ge(s_exp, at.step(g))
                V.tensor_reduce(sums[:, g % 2, :], by_window(exps[:, g % 2, :]), axis=AX, op=ALU.add).then_inc(s_sum, 1)
                dve.wait_ge(s_sum, at.step(g))
                V.reciprocal(rsum[:, g % 2, :], sums[:, g % 2, :]).then_inc(s_rsum, 1)

            def p_part(at, g):
                dve.wait_ge(s_phi, at.step(g))
                for h in range(2):
                    o = slice(64 * h, 64 * h + 64)
                    f = V.tensor_tensor(slotted(p_lo[o, g % 2, 0, :], 64 * h, P), by_window(probs[o, g % 2, :]),
                                        slotted(p_hi[o, g % 2, 0, :], 64 * h, P), ALU.subtract)
                f.then_inc(s_plo, 1)

            def v_part(at, g):
                dve.wait_ge(s_vhi, at.step(g))
                for odd in range(2):
                    for h in range(2):
                        src = ps_v[g % 2][64 * odd:64 * odd + 64, :].rearrange("p (j n) -> p j n", n=P)
                        at_h = (slice(64 * h, 64 * h + 64), g % 2, slice(odd, NW, 2), slice(DH * h, DH * h + DH))
                        f = V.scalar_tensor_tensor(v_lo[at_h], src[:, :, DH * h:DH * h + DH], 0.0, v_hi[at_h],
                                                   ALU.max, ALU.subtract)
                f.then_inc(s_vlo, 1)

            def step(at, g, last=None):
                if live(g, last):
                    if g % STEPS == AGGREGATE:
                        dve.wait_ge(s_bn, at.image(g // STEPS + 1, TILES * NCH))
                    shift(at, g)
                if live(g - LAG_SUM, last):
                    total(at, g - LAG_SUM)
                if live(g - LAG_PARTS, last):
                    p_part(at, g - LAG_PARTS)
                if live(g - LAG_V, last):
                    v_part(at, g - LAG_V)
                if live(g, last):
                    q_part(at, g + LEAD_Q)
                    if not place(g + LEAD_Q)[1]:
                        k_part(at, g + LEAD_Q)
                    for t, c in STATS.get(g % STEPS, ()):
                        stats(at, g // STEPS + 1, t, c)
                    if g % STEPS == AGGREGATE:
                        aggregate(at, g // STEPS + 1)
                    if g % STEPS == MEAN:
                        deviation(at, g // STEPS + 1)
                    if g % STEPS == VARIANCE:
                        group_variance(at, g // STEPS + 1)

            def zeros(a):
                V.memset(a, 0.0).then_inc(s_zero, 1)

            V.memset(img[:, 1, :, :], 0.0).then_inc(s_zimg, 1)
            zeros(xn_hi[:, :, :, :].bitcast(F32))
            zeros(q_hi[:, :, :].bitcast(F32))
            zeros(p_hi[:, :, :, :].bitcast(F32))
            zeros(pt[:, :, :, :].bitcast(F32))
            zero = At(0)
            for t in range(TILES):
                for c in range(NCH):
                    stats(zero, 0, t, c)
            dve.wait_ge(s_bn, TILES * NCH)
            aggregate(zero, 0)
            deviation(zero, 0)
            group_variance(zero, 0)
            dve.wait_ge(s_w, 32)
            for n, (cols, op) in enumerate((((0, 512), ALU.max), ((0, 512), ALU.min), ((512, 768), ALU.max), ((512, 768), ALU.min))):
                V.tensor_reduce(ext[:, 2 * n:2 * n + 2], w_f[:, :, cols[0]:cols[1]], axis=AX, op=op).then_inc(s_ext, 1)
            dve.wait_ge(s_all, 1)
            V.tensor_reduce(amax[:], ext_all[:].rearrange("p (a b) -> p a b", b=4), axis=AX, op=ALU.max).then_inc(s_ext, 1)
            dve.wait_ge(s_ext, 5)
            V.tensor_scalar(inv_w[:], amax[:], 1e-30, 1.0 / W_TOP, ALU.max, ALU.mult).then_inc(s_ext, 1)
            dve.wait_ge(s_ext, 6)
            V.reciprocal(mul_w[:], inv_w[:]).then_inc(s_ext, 1)
            V.tensor_tensor(sq_w[:], inv_w[:, 0:1], inv_w[:, 0:1], ALU.mult).then_inc(s_ext, 1)
            dve.wait_ge(s_ext, 8)
            V.tensor_scalar(exp_scale[:], sq_w[:], SCALE, None, ALU.mult).then_inc(s_wprep, 1)
            for n, cols in enumerate(((0, 512), (512, 768))):
                V.tensor_scalar(w_f[:, :, cols[0]:cols[1]], w_f[:, :, cols[0]:cols[1]], mul_w[:, n:n + 1], None,
                                ALU.mult).then_inc(s_ext, 1)
            dve.wait_ge(s_ext, 10)
            V.tensor_copy(w_hi[:], w_f[:]).then_inc(s_wprep, 1)
            dve.wait_ge(s_wprep, 2)
            V.tensor_tensor(w_lo[:], w_f[:], w_hi[:], ALU.subtract).then_inc(s_wprep, 1)
            for g in range(LEAD_Q):
                q_part(zero, g)
                k_part(zero, g)
            dve.wait_ge(s_zero, ZEROS)
            with dve.Fori(0, images // 2) as it:
                for g in range(2 * STEPS):
                    step(At(it), g)
            for g in range(2 * STEPS, 2 * STEPS + LAG_MIX):
                step(At(images // 2 - 1), g, 2 * STEPS)

        @block.gpsimd
        def _(pool):
            G = nc.gpsimd

            def scale_of(at, m):
                pool.wait_ge(s_gstat, at.image(m))
                G.tensor_tensor(out=norm[:, 0, :], in0=gstat[:, 1, :], in1=half[:], op=ALU.pow).then_inc(s_rstd, 1)
                pool.wait_ge(s_rstd, at.image(m))
                G.tensor_tensor(out=norm[:, 1, :], in0=gstat[:, 0, :], in1=norm[:, 0, :],
                                op=ALU.mult).then_inc(s_nmean, 1)

            def normed(at, m, n, kind, r, t, first=False):
                if first and n >= 2:
                    pool.wait_ge(s_xlo, n - 1)
                G.tensor_scalar(by_row(xt[:, n % 2, :]), windows(img[:, m % 2, t, :], kind, r),
                                norm[:, 0, t:t + 1], norm[:, 1, t:t + 1], ALU.mult, ALU.subtract).then_inc(s_xt, 1)

            def low(at, m, n, kind, r, t):
                pool.wait_ge(s_xhi, at.chunk(m, n))
                G.tensor_tensor(out=slotted(xn_lo[:, kind, t, :], r * NW * SLOT), in0=by_window(xt[:, n % 2, :]),
                                in1=slotted(xn_hi[:, kind, t, :], r * NW * SLOT), op=ALU.subtract).then_inc(s_xlo, 1)

            def add(at, g):
                m, dil, r, hp = place(g)
                pool.wait_ge(s_osb, at.step(g))
                pool.wait_ge(s_add, at.step(g - 1))
                acc = windows(img[:, m, hp, :], dil, r)
                G.tensor_tensor(out=acc, in0=by_row(o_sb[:, g % 2, :]), in1=acc, op=ALU.add).then_inc(s_add, 1)

            def divide(at, g):
                pool.wait_ge(s_rsum, at.step(g))
                pool.wait_ge(s_plo, at.step(g - 2))
                G.tensor_tensor(out=by_window(probs[:, g % 2, :]), in0=by_window(exps[:, g % 2, :]),
                                in1=rsum[:, g % 2, :].unsqueeze(2).to_broadcast([P, NW, TOK]),
                                op=ALU.mult).then_inc(s_norm, 1)

            def step(at, g, last=None):
                todo = chunks(g) if live(g, last) else []
                if todo:
                    m, n, *_ = todo[-1]
                    pool.wait_ge(s_xlo, at.chunk(m, n - 2))
                    if g % STEPS == NORMAL + 1:
                        pool.wait_ge(s_nmean, at.image(m))
                if live(g - LAG_SUM, last):
                    divide(at, g - LAG_SUM)
                for chunk in todo:
                    normed(at, *chunk)
                if g % STEPS == LAG_MIX and live(g, last):
                    pool.wait_ge(s_xt, at.chunk(g // STEPS, 31))
                add(at, g - LAG_MIX)
                for chunk in todo:
                    low(at, *chunk)
                if g % STEPS == NORMAL and live(g, last):
                    scale_of(at, g // STEPS + 1)

            G.memset(half[:], -0.5).then_inc(s_half, 1)
            G.memset(xn_lo[:, :, :, :].bitcast(F32), 0.0).then_inc(s_zero, 1)
            G.memset(q_lo[:, :, :].bitcast(F32), 0.0).then_inc(s_zero, 1)
            G.memset(p_lo[:, :, :, :].bitcast(F32), 0.0).then_inc(s_zero, 1)
            G.memset(v_hi[:, :, :, :].bitcast(F32), 0.0).then_inc(s_zero, 1)
            G.memset(v_lo[:, :, :, :].bitcast(F32), 0.0).then_inc(s_zero, 1)
            G.memset(probs[:, :, :], 0.0).then_inc(s_zero, 1)
            G.memset(exps[:, :, :], 1.0).then_inc(s_zero, 1)
            for lag, stages in ((0, (s_q, s_qhi, s_qlo, s_scores, s_max, s_shift, s_exp)),
                                (LAG_SUM, (s_sum, s_rsum, s_norm)), (LAG_PARTS, (s_phi, s_plo)),
                                (LAG_TURN, (s_turn, s_pt)), (LAG_V, (s_v, s_vhi, s_vlo)),
                                (LAG_MIX, (s_mix, s_osb, s_add))):
                for s in stages:
                    pool.sem_inc(s, AHEAD - lag)
            pool.wait_ge(s_half, 1)
            pool.wait_ge(s_ext, 4)
            G.partition_all_reduce(ext_all[:], ext[:], P, bass.bass_isa.ReduceOp.absmax).then_inc(s_all, 1)
            zero = At(0)
            scale_of(zero, 0)
            pool.wait_ge(s_nmean, 1)
            for n, (step_, kind, r, t) in enumerate(ORDER):
                if step_ < STEPS:
                    normed(zero, 0, n, kind, r, t, True)
                    low(zero, 0, n, kind, r, t)
            with pool.Fori(0, images // 2) as it:
                for g in range(2 * STEPS):
                    step(At(it), g)
            for g in range(2 * STEPS, 2 * STEPS + LAG_MIX):
                step(At(images // 2 - 1), g, 2 * STEPS)


def kernel(x, L0_conv_qk_w, L0_conv_v_w):
    import numpy as np
    import concourse.bacc as bacc
    from concourse.bass_utils import run_bass_kernel_spmd

    sel = np.zeros((P, TOK), np.float16)
    for h in range(2):
        for a in range(WS):
            for b in range(WS):
                sel[SLOT * h + WS * a + b, WS * a + b] = 1
    grp = np.kron(np.eye(P // 8), np.full((8, 8), 0.125)).astype(np.float32)
    nc = bacc.Bacc("TRN2", target_bir_lowering=False, num_devices=1)
    arrays = {
        "x_dram": np.ascontiguousarray(x),
        "qk_wt_dram": np.ascontiguousarray(np.asarray(L0_conv_qk_w).T),
        "v_wt_dram": np.ascontiguousarray(np.asarray(L0_conv_v_w).T),
        "sel_dram": sel,
        "grp_dram": grp,
    }
    args = [nc.dram_tensor(n, a.shape, mybir.dt.from_np(a.dtype), kind="ExternalInput").ap()
            for n, a in arrays.items()]
    out = nc.dram_tensor("out_dram", arrays["x_dram"].shape, F32, kind="ExternalOutput").ap()
    window_attention(nc, *args, out)
    r = run_bass_kernel_spmd(nc, [arrays], core_ids=[0])
    return r.results[0]["out_dram"]
```

```python
import concourse.bass as bass
from concourse import mybir
from contextlib import ExitStack

F32 = mybir.dt.float32
F16 = mybir.dt.float16
ALU = mybir.AluOpType
ACT = mybir.ActivationFunctionType
AX = mybir.AxisListType.X

WS = 7
SIDE = 56
NW = SIDE // WS
PIX = SIDE * SIDE
TOK = WS * WS
SLOT = 64
P = 128
HEADS, DH = 4, 64
TILES = 2
GROUP = NW * TOK
STEPS = 32
ZEROS = 14
LAG_SCORES, LAG_MAX, LAG_SHIFT = 0, 0, 0
LAG_EXP, LAG_SUM, LAG_DIVIDE = 1, 1, 2
LAG_P = 3
LAG_V = 3
LAG_TURN, LAG_PT = 5, 5
LAG_MIX, LAG_OSB, LAG_ADD = 6, 5, 6
LAG_Q, LAG_K = -2, -3
FIRST = -3
MOST = 6
AHEAD = 10
CH = 448
NCH = PIX // CH
W_TOP = 4.0
GN_EPS = 1e-5
SCALE = DH ** -0.5


def view(a, offset, dims):
    return bass.AP(a.tensor, a.offset + offset, [list(a.ap[0]), *[list(d) for d in dims]])


def window_attention(nc, x, qk_wt, v_wt, sel, grp, out):
    images = x.shape[0]
    x_d = x.rearrange("b (t p) h w -> b t p (h w)", p=P)
    out_d = out.rearrange("b (t p) h w -> b t p (h w)", p=P)

    ctx = ExitStack()
    with ctx:
        def sb(name, shape, dt):
            return ctx.enter_context(nc.sbuf_tensor(name, shape, dt))

        def pb(name, shape, dt=F32):
            return ctx.enter_context(nc.psum_tensor(name, shape, dt))

        def sem(name):
            return ctx.enter_context(nc.semaphore(name))

        img = sb("img", [P, 2, TILES, PIX], F32)
        xn_hi = sb("xn_hi", [P, 2, TILES, NW * NW * SLOT], F16)
        xn_lo = sb("xn_lo", [P, 2, TILES, NW * NW * SLOT], F16)
        q_hi = sb("q_hi", [P, 2, NW, P], F16)
        q_lo = sb("q_lo", [P, 2, NW, P], F16)
        k_hi = sb("k_hi", [P, 2, PIX], F16)
        k_lo = sb("k_lo", [P, 2, PIX], F16)
        w_f = sb("w_f", [P, TILES, 768], F32)
        w_hi = sb("w_hi", [P, TILES, 768], F16)
        w_lo = sb("w_lo", [P, TILES, 768], F16)
        select = sb("select", [P, TOK], F16)
        group_mean = sb("group_mean", [P, P], F32)
        smax = sb("smax", [P, 2, NW], F32)
        shifted = sb("shifted", [P, 2, GROUP], F32)
        exps = sb("exps", [P, 2, GROUP], F32)
        sums = sb("sums", [P, 2, NW], F32)
        rsum = sb("rsum", [P, 2, NW], F32)
        probs = sb("probs", [P, 2, GROUP], F32)
        p_hi = sb("p_hi", [P, 2, NW, P], F16)
        p_lo = sb("p_lo", [P, 2, NW, P], F16)
        pt = sb("pt", [P, 2, 2, GROUP], F16)
        v_hi = sb("v_hi", [P, 2, NW, P], F16)
        v_lo = sb("v_lo", [P, 2, NW, P], F16)
        o_sb = sb("o_sb", [P, 2, GROUP], F32)
        bn = sb("bn", [P, TILES, NCH, 6], F32)
        mv = sb("mv", [P, 2, TILES], F32)
        dev = sb("dev", [P, 3, TILES], F32)
        gstat = sb("gstat", [P, 2, TILES], F32)
        norm = sb("norm", [P, 2, TILES], F32)
        xt = sb("xt", [P, 2, GROUP], F32)
        ext = sb("ext", [P, 8], F32)
        ext_all = sb("ext_all", [P, 8], F32)
        amax = sb("amax", [P, 2], F32)
        inv_w = sb("inv_w", [P, 2], F32)
        rec_w = sb("rec_w", [P, 2], F32)
        mul_w = sb("mul_w", [P, 2], F32)
        sq_w = sb("sq_w", [P, 1], F32)
        exp_scale = sb("exp_scale", [P, 1], F32)
        v_scale = inv_w[:, 1:2]
        half = sb("half", [P, TILES], F32)

        ps_s = pb("ps_s", [P, 512])
        ps_q = pb("ps_q", [P, 512])
        ps_k = pb("ps_k", [P, 512])
        ps_v = [pb(f"ps_v{i}", [P, 512]) for i in range(2)]
        ps_t = pb("ps_t", [P, 2, 512])
        ps_o = pb("ps_o", [P, 512])
        ps_g = ps_k[:, 448:452]

        s_scores, s_max, s_shift, s_exp, s_sum, s_rsum, s_norm = map(
            sem, ("s_scores", "s_max", "s_shift", "s_exp", "s_sum", "s_rsum", "s_norm"))
        s_phi, s_plo_a, s_plo_b, s_turn, s_pt, s_v, s_vhi, s_vlo, s_mix, s_osb, s_add = map(
            sem, ("s_phi", "s_plo_a", "s_plo_b", "s_turn", "s_pt", "s_v", "s_vhi", "s_vlo", "s_mix", "s_osb", "s_add"))
        s_q, s_k, s_qhi, s_qlo, s_khi, s_klo = map(sem, ("s_q", "s_k", "s_qhi", "s_qlo", "s_khi", "s_klo"))
        s_bn, s_mv, s_mean, s_dev1, s_dev2, s_dev, s_var, s_gstat, s_rstd, s_nmean = map(
            sem, ("s_bn", "s_mv", "s_mean", "s_dev1", "s_dev2", "s_dev", "s_var", "s_gstat", "s_rstd", "s_nmean"))
        s_xt, s_xhi, s_xlo = map(sem, ("s_xt", "s_xhi", "s_xlo"))
        s_load = [sem(f"s_load{t}") for t in range(TILES)]
        s_store = [sem(f"s_store{t}") for t in range(TILES)]
        s_const, s_zero, s_zimg, s_half, s_ext, s_all, s_w, s_wprep = map(
            sem, ("s_const", "s_zero", "s_zimg", "s_half", "s_ext", "s_all", "s_w", "s_wprep"))

        block = ctx.enter_context(nc.Block())

        class At:

            def __init__(self, it):
                self.it = it

            def step(self, g):
                return self.it * (2 * STEPS) + (AHEAD + g + 1)

            def keys(self, g):
                return self.it * 32 + (16 * (g // STEPS) + g % STEPS + 1)

            def image(self, m, per=1):
                return self.it * (2 * per) + (m + 1) * per

            def chunk(self, m, n):
                return self.it * 64 + (32 * m + n + 1)

        def place(g):
            s = g % STEPS
            return (g // STEPS) % 2, s // 16, (s // 2) % 8, s % 2

        def due(j, span):
            return span is None or span[0] <= j < span[1]

        def windows(a, dilated, r):
            if dilated:
                return view(a, SIDE * r, [[1, NW], [NW * SIDE, WS], [NW, WS]])
            return view(a, WS * SIDE * r, [[WS, NW], [SIDE, WS], [1, WS]])

        def tokens(a, dilated, r, w):
            if dilated:
                return view(a, SIDE * r + w, [[NW * SIDE, WS], [NW, WS]])
            return view(a, WS * SIDE * r + WS * w, [[SIDE, WS], [1, WS]])

        def slotted(a, first=0, pitch=SLOT):
            return view(a, first, [[pitch, NW], [1, TOK]])

        def by_window(a):
            return a.rearrange("p (w t) -> p w t", t=TOK)

        def by_row(a):
            return a.rearrange("p (w a b) -> p w a b", w=NW, b=WS)

        STATS = {10: [(0, 0), (0, 1), (0, 2)], 11: [(0, 3), (0, 4)], 12: [(0, 5), (0, 6)],
                 13: [(1, 0), (1, 1), (1, 2)], 14: [(1, 3), (1, 4)], 15: [(1, 5), (1, 6)]}
        AGGREGATE, MEAN, VARIANCE = 16, 17, 18
        FIRST_CHUNK, SPREAD = 19, 18.8
        ORDER = [(int(FIRST_CHUNK + SPREAD * n / 31), n // 16, n % 16 // 2, n % 2) for n in range(32)]
        assert all(step - LAG_V >= 16 * kind + 2 * r + 1 for step, kind, r, t in ORDER)
        assert ORDER[31][0] < STEPS + LAG_ADD
        BEFORE = sum(step < STEPS for step, *_ in ORDER)

        def chunk_of(dil, r):
            return 16 * dil + 2 * r + 1

        def chunks(g, first, span):
            s = g % STEPS
            found = [(g // STEPS + (step < STEPS), n, kind, r, t) for n, (step, kind, r, t) in enumerate(ORDER)
                     if step % STEPS == s and due(g, span)]
            return found[:1] if first else found[1:]

        @block.sync
        def _(sp):
            def load(i, t, par):
                sp.dma_start(img[:, par, t, :], x_d[i, t]).then_inc(s_load[t], 16)

            def store(i, t, par):
                sp.dma_start(out_d[i, t], img[:, par, t, :]).then_inc(s_store[t], 16)

            for t in range(TILES):
                load(0, t, 0)
            sp.wait_ge(s_zimg, 1)
            sp.wait_ge(s_add, AHEAD)
            for t in range(TILES):
                load(1, t, 1)

            def image(at, m, nxt):
                sp.wait_ge(s_add, at.step(m * STEPS + STEPS - 1))
                for t in range(TILES):
                    store(at.it * 2 + m, t, m)
                if nxt is not None:
                    for t in range(TILES):
                        sp.wait_ge(s_store[t], at.it * 32 + 16 * (m + 1))
                        load(nxt, t, m)

            with sp.Fori(0, images // 2 - 1) as it:
                for m in range(2):
                    image(At(it), m, it * 2 + (m + 2))
            image(At(images // 2 - 1), 0, images - 1)
            image(At(images // 2 - 1), 1, None)
            for t in range(TILES):
                sp.wait_ge(s_store[t], 16 * images)

        @block.tensor
        def _(pe):
            mm = nc.tensor.matmul

            def three(o, stat, mov, first, last):
                mm(o, stat[0], mov[0], start=first, stop=False)
                mm(o, stat[0], mov[1], start=False, stop=False)
                return mm(o, stat[1], mov[0], start=False, stop=last)

            def project(bank, dil, r, hp, col):
                for c in range(TILES):
                    w = slice(col + P * hp, col + P * hp + P)
                    mov = [slotted(a[:, dil, c, :], r * NW * SLOT) for a in (xn_hi, xn_lo)]
                    last = three(bank[:, 0:GROUP], (w_hi[:, c, w], w_lo[:, c, w]), mov, c == 0, c == TILES - 1)
                return last

            def project_q(at, g):
                m, dil, r, hp = place(g)
                if dil:
                    pe.wait_ge(s_xlo, at.chunk(g // STEPS, chunk_of(dil, r)))
                pe.wait_ge(s_qlo, at.step(g - 1))
                project(ps_q, dil, r, hp, 0).then_inc(s_q, 1)

            def project_k(at, g, wait=True):
                m, dil, r, hp = place(g)
                if hp == 0:
                    pe.wait_ge(s_xlo, at.chunk(g // STEPS, chunk_of(dil, r)))
                if wait:
                    pe.wait_ge(s_klo, at.keys(g) - 1)
                project(ps_k, dil, r, hp, 256).then_inc(s_k, 1)

            def mean(at, m):
                pe.wait_ge(s_mv, at.image(m))
                mm(ps_g[:, 0:2], group_mean[:], mv[:, 0, :], start=True, stop=True).then_inc(s_mean, 1)

            def variance(at, m):
                pe.wait_ge(s_dev, at.image(m))
                mm(ps_g[:, 2:4], group_mean[:], dev[:, 2, :], start=True, stop=True).then_inc(s_var, 1)

            def scores(at, g):
                m, dil, r, hp = place(g)
                pe.wait_ge(s_qlo, at.step(g))
                if not dil:
                    pe.wait_ge(s_klo, at.keys(g))
                pe.wait_ge(s_shift, at.step(g - 1))
                for w in range(NW):
                    f = three(ps_s[:, w * TOK:w * TOK + TOK], (q_hi[:, g % 2, w, :], q_lo[:, g % 2, w, :]),
                              [tokens(a[:, hp, :], dil, r, w) for a in (k_hi, k_lo)], True, True)
                f.then_inc(s_scores, 1)

            def turn(at, g):
                pe.wait_ge(s_plo_a, at.step(g))
                pe.wait_ge(s_plo_b, at.step(g))
                pe.wait_ge(s_pt, at.step(g - 1))
                for k, part in enumerate((p_hi, p_lo)):
                    for w in range(NW):
                        f = mm(ps_t[:, k, w * TOK:w * TOK + TOK], part[:, g % 2, w, :], select[:],
                               start=True, stop=True)
                f.then_inc(s_turn, 1)

            def values(at, g):
                m, dil, r, hp = place(g)
                pe.wait_ge(s_vlo, at.step(g - 2))
                cols = slice(512 + P * hp, 512 + P * hp + P)
                for w in range(0, NW, 2):
                    for c in range(TILES):
                        at_w = slice((r * NW + w) * SLOT, (r * NW + w + 2) * SLOT)
                        f = three(ps_v[g % 2][:, w * DH:w * DH + P], [a[:, dil, c, at_w] for a in (xn_hi, xn_lo)],
                                  (w_hi[:, c, cols], w_lo[:, c, cols]), c == 0, c == TILES - 1)
                f.then_inc(s_v, 1)

            def mix(at, g):
                pe.wait_ge(s_osb, at.step(g - 1))
                pe.wait_ge(s_pt, at.step(g))
                pe.wait_ge(s_vlo, at.step(g))
                for w in range(NW):
                    t = slice(w * TOK, w * TOK + TOK)
                    f = three(ps_o[:, t], (v_hi[:, g % 2, w, :], v_lo[:, g % 2, w, :]),
                              (pt[:, g % 2, 0, t], pt[:, g % 2, 1, t]), True, True)
                f.then_inc(s_mix, 1)

            def step(at, g, span=None):
                if due(g - LAG_MIX, span):
                    mix(at, g - LAG_MIX)
                if due(g - LAG_TURN, span):
                    turn(at, g - LAG_TURN)
                if g % STEPS == MEAN and due(g, span):
                    mean(at, g // STEPS + 1)
                if g % STEPS == VARIANCE and due(g, span):
                    variance(at, g // STEPS + 1)
                if due(g - LAG_V, span):
                    values(at, g - LAG_V)
                if due(g - LAG_SCORES, span):
                    scores(at, g - LAG_SCORES)
                if due(g - LAG_Q, span):
                    project_q(at, g - LAG_Q)
                if due(g - LAG_K, span) and not place(g - LAG_K)[1]:
                    project_k(at, g - LAG_K, g > LAG_K)

            zero = At(0)
            pe.wait_ge(s_const, 32)
            mean(zero, 0)
            variance(zero, 0)
            pe.wait_ge(s_wprep, 3)
            pe.wait_ge(s_zero, ZEROS)
            for g in range(FIRST, 0):
                step(zero, g, (0, STEPS))
            pe.wait_ge(s_xlo, BEFORE)
            with pe.Fori(0, images // 2) as it:
                for g in range(2 * STEPS):
                    step(At(it), g)
            for g in range(2 * STEPS, 2 * STEPS + MOST):
                step(At(images // 2 - 1), g, (0, 2 * STEPS))

        @block.scalar
        def _(act):
            def copy(o, i):
                return nc.scalar.activation(o, i, ACT.Copy)

            def q_part(at, g):
                act.wait_ge(s_q, at.step(g))
                for h in range(2):
                    o = slice(64 * h, 64 * h + 64)
                    f = copy(slotted(q_hi[o, g % 2, 0, :], 64 * h, P), by_window(ps_q[o, 0:GROUP]))
                f.then_inc(s_qhi, 1)

            def k_part(at, g):
                m, dil, r, hp = place(g)
                act.wait_ge(s_k, at.keys(g))
                copy(windows(k_hi[:, hp, :], dil, r), by_row(ps_k[:, 0:GROUP])).then_inc(s_khi, 1)

            def x_part(at, m, n, kind, r, t):
                act.wait_ge(s_xt, at.chunk(m, n))
                copy(slotted(xn_hi[:, kind, t, :], r * NW * SLOT), by_window(xt[:, n % 2, :])).then_inc(s_xhi, 1)

            def p_part(at, g):
                act.wait_ge(s_norm, at.step(g))
                for h in range(2):
                    o = slice(64 * h, 64 * h + 64)
                    f = copy(slotted(p_hi[o, g % 2, 0, :], 64 * h, P), by_window(probs[o, g % 2, :]))
                f.then_inc(s_phi, 1)

            def turned(at, g):
                act.wait_ge(s_turn, at.step(g))
                copy(pt[:, g % 2, :, :], ps_t[:, :, 0:GROUP]).then_inc(s_pt, 1)

            def exp(at, g):
                act.wait_ge(s_shift, at.step(g))
                nc.scalar.activation(exps[:, g % 2, :], shifted[:, g % 2, :], ACT.Exp,
                                     scale=exp_scale[:, 0:1]).then_inc(s_exp, 1)

            def mixed(at, g):
                act.wait_ge(s_mix, at.step(g))
                act.wait_ge(s_add, at.step(g - 2))
                nc.scalar.activation(o_sb[:, g % 2, :], ps_o[:, 0:GROUP], ACT.Copy,
                                     scale=v_scale).then_inc(s_osb, 1)

            def v_part(at, g):
                act.wait_ge(s_v, at.step(g))
                for odd in range(2):
                    for h in range(2):
                        src = ps_v[g % 2][64 * odd:64 * odd + 64, :].rearrange("p (j n) -> p j n", n=P)
                        f = nc.scalar.activation(v_hi[64 * h:64 * h + 64, g % 2, odd::2, DH * h:DH * h + DH],
                                                 src[:, :, DH * h:DH * h + DH], ACT.Relu)
                f.then_inc(s_vhi, 1)

            def step(at, g, span=None):
                if due(g - LAG_PT, span):
                    turned(at, g - LAG_PT)
                if due(g - LAG_P, span):
                    p_part(at, g - LAG_P)
                if due(g - LAG_EXP, span):
                    exp(at, g - LAG_EXP)
                if due(g - LAG_Q, span):
                    q_part(at, g - LAG_Q)
                if due(g - LAG_K, span) and not place(g - LAG_K)[1]:
                    k_part(at, g - LAG_K)
                if due(g - LAG_OSB, span):
                    mixed(at, g - LAG_OSB)
                if due(g - LAG_V, span):
                    v_part(at, g - LAG_V)
                for first in (True, False):
                    for chunk in chunks(g, first, span):
                        x_part(at, *chunk)

            act.dma_start(w_f[:, :, 0:512], qk_wt.rearrange("(t p) n -> p t n", p=P)).then_inc(s_w, 16)
            act.dma_start(w_f[:, :, 512:768], v_wt.rearrange("(t p) n -> p t n", p=P)).then_inc(s_w, 16)
            act.dma_start(select[:], sel).then_inc(s_const, 16)
            act.dma_start(group_mean[:], grp).then_inc(s_const, 16)
            zero = At(0)
            act.wait_ge(s_zero, ZEROS)
            for n, (_, kind, r, t) in enumerate(ORDER[:BEFORE]):
                x_part(zero, 0, n, kind, r, t)
            for g in range(FIRST, 0):
                step(zero, g, (0, STEPS))
            act.wait_ge(s_wprep, 3)
            with act.Fori(0, images // 2) as it:
                for g in range(2 * STEPS):
                    step(At(it), g)
            for g in range(2 * STEPS, 2 * STEPS + MOST):
                step(At(images // 2 - 1), g, (0, 2 * STEPS))

        @block.vector
        def _(dve):
            V = nc.vector

            def q_part(at, g):
                dve.wait_ge(s_qhi, at.step(g))
                for h in range(2):
                    o = slice(64 * h, 64 * h + 64)
                    f = V.tensor_tensor(slotted(q_lo[o, g % 2, 0, :], 64 * h, P), by_window(ps_q[o, 0:GROUP]),
                                        slotted(q_hi[o, g % 2, 0, :], 64 * h, P), ALU.subtract)
                f.then_inc(s_qlo, 1)

            def k_part(at, g):
                m, dil, r, hp = place(g)
                dve.wait_ge(s_khi, at.keys(g))
                V.tensor_tensor(windows(k_lo[:, hp, :], dil, r), by_row(ps_k[:, 0:GROUP]),
                                windows(k_hi[:, hp, :], dil, r), ALU.subtract).then_inc(s_klo, 1)

            def stats(at, m, t, c):
                if c == 0:
                    dve.wait_ge(s_load[t], at.image(m, 16))
                V.bn_stats(bn[:, t, c, :], img[:, m % 2, t, c * CH:c * CH + CH]).then_inc(s_bn, 1)

            def aggregate(at, m):
                for t in range(TILES):
                    f = V.bn_aggr(mv[:, :, t], bn[:, t, :, :])
                f.then_inc(s_mv, 1)

            def deviation(at, m):
                dve.wait_ge(s_mean, at.image(m))
                V.tensor_tensor(dev[:, 0, :], ps_g[:, 0:2], mv[:, 0, :], ALU.subtract)
                V.tensor_scalar(gstat[:, 0, :], ps_g[:, 0:2], -1.0, None, ALU.mult).then_inc(s_dev1, 1)
                dve.wait_ge(s_dev1, at.image(m))
                V.tensor_tensor(dev[:, 1, :], dev[:, 0, :], dev[:, 0, :], ALU.mult).then_inc(s_dev2, 1)
                dve.wait_ge(s_dev2, at.image(m))
                V.tensor_tensor(dev[:, 2, :], dev[:, 1, :], mv[:, 1, :], ALU.add).then_inc(s_dev, 1)

            def group_variance(at, m):
                dve.wait_ge(s_var, at.image(m))
                V.tensor_scalar(gstat[:, 1, :], ps_g[:, 2:4], GN_EPS, None, ALU.add).then_inc(s_gstat, 1)

            def largest(at, g):
                dve.wait_ge(s_scores, at.step(g))
                V.tensor_reduce(smax[:, g % 2, :], by_window(ps_s[:, 0:GROUP]), axis=AX, op=ALU.max).then_inc(s_max, 1)

            def shift(at, g):
                dve.wait_ge(s_max, at.step(g))
                V.tensor_tensor(by_window(shifted[:, g % 2, :]), by_window(ps_s[:, 0:GROUP]),
                                smax[:, g % 2, :].unsqueeze(2).to_broadcast([P, NW, TOK]),
                                ALU.subtract).then_inc(s_shift, 1)

            def total(at, g):
                dve.wait_ge(s_exp, at.step(g))
                V.tensor_reduce(sums[:, g % 2, :], by_window(exps[:, g % 2, :]), axis=AX, op=ALU.add).then_inc(s_sum, 1)

            def inverse(at, g):
                dve.wait_ge(s_sum, at.step(g))
                V.reciprocal(rsum[:, g % 2, :], sums[:, g % 2, :]).then_inc(s_rsum, 1)

            def p_part(at, g):
                o = slice(64, P)
                dve.wait_ge(s_phi, at.step(g))
                V.tensor_tensor(slotted(p_lo[o, g % 2, 0, :], 64, P), by_window(probs[o, g % 2, :]),
                                slotted(p_hi[o, g % 2, 0, :], 64, P), ALU.subtract).then_inc(s_plo_b, 1)

            def normed(at, m, n, kind, r, t, first=False):
                if n == 0:
                    dve.wait_ge(s_nmean, at.image(m))
                if not first or n >= 2:
                    dve.wait_ge(s_xlo, at.chunk(m, n - 2))
                V.tensor_scalar(by_row(xt[:, n % 2, :]), windows(img[:, m % 2, t, :], kind, r), norm[:, 0, t:t + 1],
                                norm[:, 1, t:t + 1], ALU.mult, ALU.add).then_inc(s_xt, 1)

            def v_part(at, g):
                dve.wait_ge(s_vhi, at.step(g))
                for odd in range(2):
                    for h in range(2):
                        src = ps_v[g % 2][64 * odd:64 * odd + 64, :].rearrange("p (j n) -> p j n", n=P)
                        at_h = (slice(64 * h, 64 * h + 64), g % 2, slice(odd, NW, 2), slice(DH * h, DH * h + DH))
                        f = V.scalar_tensor_tensor(v_lo[at_h], src[:, :, DH * h:DH * h + DH], 0.0, v_hi[at_h],
                                                   ALU.max, ALU.subtract)
                f.then_inc(s_vlo, 1)

            def step(at, g, span=None):
                if g % STEPS == AGGREGATE and due(g, span):
                    dve.wait_ge(s_bn, at.image(g // STEPS + 1, TILES * NCH))
                if due(g - LAG_MAX, span):
                    largest(at, g - LAG_MAX)
                if due(g - LAG_SUM, span):
                    total(at, g - LAG_SUM)
                if due(g - LAG_SHIFT, span):
                    shift(at, g - LAG_SHIFT)
                if due(g, span):
                    for t, c in STATS.get(g % STEPS, ()):
                        stats(at, g // STEPS + 1, t, c)
                    if g % STEPS == AGGREGATE:
                        aggregate(at, g // STEPS + 1)
                for chunk in chunks(g, True, span):
                    normed(at, *chunk)
                if due(g - LAG_Q, span):
                    q_part(at, g - LAG_Q)
                if due(g - LAG_P, span):
                    p_part(at, g - LAG_P)
                if due(g - LAG_SUM, span):
                    inverse(at, g - LAG_SUM)
                if due(g - LAG_K, span) and not place(g - LAG_K)[1]:
                    k_part(at, g - LAG_K)
                if due(g, span):
                    if g % STEPS == MEAN:
                        deviation(at, g // STEPS + 1)
                    if g % STEPS == VARIANCE:
                        group_variance(at, g // STEPS + 1)
                for chunk in chunks(g, False, span):
                    normed(at, *chunk)
                if due(g - LAG_V, span):
                    v_part(at, g - LAG_V)

            def zeros(a):
                V.memset(a, 0.0).then_inc(s_zero, 1)

            V.memset(img[:, 1, :, :], 0.0).then_inc(s_zimg, 1)
            zeros(xn_hi[:, :, :, :].bitcast(F32))
            zeros(q_hi[:, :, :].bitcast(F32))
            zeros(p_hi[:, :, :, :].bitcast(F32))
            zeros(pt[:, :, :, :].bitcast(F32))
            zeros(shifted[:, :, :])
            zeros(rsum[:, :, :])
            zeros(o_sb[:, :, :])
            zero = At(0)
            for t in range(TILES):
                for c in range(NCH):
                    stats(zero, 0, t, c)
            dve.wait_ge(s_bn, TILES * NCH)
            aggregate(zero, 0)
            deviation(zero, 0)
            group_variance(zero, 0)
            dve.wait_ge(s_w, 32)
            for n, (cols, op) in enumerate((((0, 512), ALU.max), ((0, 512), ALU.min), ((512, 768), ALU.max), ((512, 768), ALU.min))):
                V.tensor_reduce(ext[:, 2 * n:2 * n + 2], w_f[:, :, cols[0]:cols[1]], axis=AX, op=op).then_inc(s_ext, 1)
            dve.wait_ge(s_all, 1)
            V.tensor_reduce(amax[:], ext_all[:].rearrange("p (a b) -> p a b", b=4), axis=AX, op=ALU.max).then_inc(s_ext, 1)
            dve.wait_ge(s_ext, 5)
            V.tensor_scalar(inv_w[:], amax[:], 1e-30, 1.0 / W_TOP, ALU.max, ALU.mult).then_inc(s_ext, 1)
            dve.wait_ge(s_ext, 6)
            V.reciprocal(mul_w[:], inv_w[:]).then_inc(s_ext, 1)
            V.tensor_tensor(sq_w[:], inv_w[:, 0:1], inv_w[:, 0:1], ALU.mult).then_inc(s_ext, 1)
            dve.wait_ge(s_ext, 8)
            V.tensor_scalar(exp_scale[:], sq_w[:], SCALE, None, ALU.mult).then_inc(s_wprep, 1)
            for n, cols in enumerate(((0, 512), (512, 768))):
                V.tensor_scalar(w_f[:, :, cols[0]:cols[1]], w_f[:, :, cols[0]:cols[1]], mul_w[:, n:n + 1], None,
                                ALU.mult).then_inc(s_ext, 1)
            dve.wait_ge(s_ext, 10)
            V.tensor_copy(w_hi[:], w_f[:]).then_inc(s_wprep, 1)
            dve.wait_ge(s_wprep, 2)
            V.tensor_tensor(w_lo[:], w_f[:], w_hi[:], ALU.subtract).then_inc(s_wprep, 1)
            dve.wait_ge(s_zero, ZEROS)
            for n, (_, kind, r, t) in enumerate(ORDER[:BEFORE]):
                normed(zero, 0, n, kind, r, t, True)
            for g in range(FIRST, 0):
                step(zero, g, (0, STEPS))
            with dve.Fori(0, images // 2) as it:
                for g in range(2 * STEPS):
                    step(At(it), g)
            for g in range(2 * STEPS, 2 * STEPS + MOST):
                step(At(images // 2 - 1), g, (0, 2 * STEPS))

        @block.gpsimd
        def _(pool):
            G = nc.gpsimd

            def scale_of(at, m):
                pool.wait_ge(s_gstat, at.image(m))
                G.tensor_tensor(out=norm[:, 0, :], in0=gstat[:, 1, :], in1=half[:], op=ALU.pow).then_inc(s_rstd, 1)
                pool.wait_ge(s_rstd, at.image(m))
                G.tensor_tensor(out=norm[:, 1, :], in0=gstat[:, 0, :], in1=norm[:, 0, :],
                                op=ALU.mult).then_inc(s_nmean, 1)

            def low(at, m, n, kind, r, t):
                pool.wait_ge(s_xhi, at.chunk(m, n))
                G.tensor_tensor(out=slotted(xn_lo[:, kind, t, :], r * NW * SLOT), in0=by_window(xt[:, n % 2, :]),
                                in1=slotted(xn_hi[:, kind, t, :], r * NW * SLOT), op=ALU.subtract).then_inc(s_xlo, 1)

            def add(at, g):
                m, dil, r, hp = place(g)
                pool.wait_ge(s_osb, at.step(g))
                pool.wait_ge(s_add, at.step(g - 1))
                acc = windows(img[:, m, hp, :], dil, r)
                G.tensor_tensor(out=acc, in0=by_row(o_sb[:, g % 2, :]), in1=acc, op=ALU.add).then_inc(s_add, 1)

            def divide(at, g):
                pool.wait_ge(s_rsum, at.step(g))
                pool.wait_ge(s_plo_a, at.step(g - 2))
                G.tensor_tensor(out=by_window(probs[:, g % 2, :]), in0=by_window(exps[:, g % 2, :]),
                                in1=rsum[:, g % 2, :].unsqueeze(2).to_broadcast([P, NW, TOK]),
                                op=ALU.mult).then_inc(s_norm, 1)

            def p_part(at, g):
                o = slice(0, 64)
                pool.wait_ge(s_phi, at.step(g))
                G.tensor_tensor(out=slotted(p_lo[o, g % 2, 0, :], 0, P), in0=by_window(probs[o, g % 2, :]),
                                in1=slotted(p_hi[o, g % 2, 0, :], 0, P), op=ALU.subtract).then_inc(s_plo_a, 1)

            def step(at, g, span=None):
                if due(g - LAG_DIVIDE, span):
                    divide(at, g - LAG_DIVIDE)
                if due(g - LAG_P, span):
                    p_part(at, g - LAG_P)
                for chunk in chunks(g, True, span):
                    low(at, *chunk)
                if due(g - LAG_ADD, span):
                    add(at, g - LAG_ADD)
                for chunk in chunks(g, False, span):
                    low(at, *chunk)
                if g % STEPS == VARIANCE and due(g, span):
                    scale_of(at, g // STEPS + 1)

            G.memset(half[:], -0.5).then_inc(s_half, 1)
            G.memset(xn_lo[:, :, :, :].bitcast(F32), 0.0).then_inc(s_zero, 1)
            G.memset(q_lo[:, :, :].bitcast(F32), 0.0).then_inc(s_zero, 1)
            G.memset(p_lo[:, :, :, :].bitcast(F32), 0.0).then_inc(s_zero, 1)
            G.memset(v_hi[:, :, :, :].bitcast(F32), 0.0).then_inc(s_zero, 1)
            G.memset(v_lo[:, :, :, :].bitcast(F32), 0.0).then_inc(s_zero, 1)
            G.memset(probs[:, :, :], 0.0).then_inc(s_zero, 1)
            G.memset(exps[:, :, :], 1.0).then_inc(s_zero, 1)
            for lag, stages in ((LAG_SCORES, (s_q, s_qhi, s_qlo, s_scores, s_max, s_shift)),
                                (LAG_EXP, (s_exp, s_sum, s_rsum)), (LAG_DIVIDE, (s_norm,)),
                                (LAG_P, (s_phi, s_plo_a, s_plo_b)), (LAG_V, (s_v, s_vhi, s_vlo)), (LAG_TURN, (s_turn, s_pt)),
                                (LAG_MIX, (s_mix, s_add)), (LAG_OSB, (s_osb,))):
                for s in stages:
                    pool.sem_inc(s, AHEAD - lag)
            pool.wait_ge(s_half, 1)
            pool.wait_ge(s_ext, 4)
            G.partition_all_reduce(ext_all[:], ext[:], P, bass.bass_isa.ReduceOp.absmax).then_inc(s_all, 1)
            zero = At(0)
            scale_of(zero, 0)
            for n, (_, kind, r, t) in enumerate(ORDER[:BEFORE]):
                low(zero, 0, n, kind, r, t)
            with pool.Fori(0, images // 2) as it:
                for g in range(2 * STEPS):
                    step(At(it), g)
            for g in range(2 * STEPS, 2 * STEPS + MOST):
                step(At(images // 2 - 1), g, (0, 2 * STEPS))


def kernel(x, L0_conv_qk_w, L0_conv_v_w):
    import numpy as np
    import concourse.bacc as bacc
    from concourse.bass_utils import run_bass_kernel_spmd

    sel = np.zeros((P, TOK), np.float16)
    for h in range(2):
        for a in range(WS):
            for b in range(WS):
                sel[SLOT * h + WS * a + b, WS * a + b] = 1
    grp = np.kron(np.eye(P // 8), np.full((8, 8), 0.125)).astype(np.float32)
    nc = bacc.Bacc("TRN2", target_bir_lowering=False, num_devices=1)
    arrays = {
        "x_dram": np.ascontiguousarray(x),
        "qk_wt_dram": np.ascontiguousarray(np.asarray(L0_conv_qk_w).T),
        "v_wt_dram": np.ascontiguousarray(np.asarray(L0_conv_v_w).T),
        "sel_dram": sel,
        "grp_dram": grp,
    }
    args = [nc.dram_tensor(n, a.shape, mybir.dt.from_np(a.dtype), kind="ExternalInput").ap()
            for n, a in arrays.items()]
    out = nc.dram_tensor("out_dram", arrays["x_dram"].shape, F32, kind="ExternalOutput").ap()
    window_attention(nc, *args, out)
    r = run_bass_kernel_spmd(nc, [arrays], core_ids=[0])
    return r.results[0]["out_dram"]
```

```python
import concourse.bass as bass
from concourse import mybir
from contextlib import ExitStack

F32 = mybir.dt.float32
F16 = mybir.dt.float16
ALU = mybir.AluOpType
ACT = mybir.ActivationFunctionType
AX = mybir.AxisListType.X

WS = 7
SIDE = 56
NW = SIDE // WS
PIX = SIDE * SIDE
TOK = WS * WS
SLOT = 64
P = 128
DH = 64
TILES = 2
GROUP = NW * TOK
STEPS = 32
ZEROS = 15
LAG_SCORES, LAG_MAX, LAG_SHIFT = 0, 0, 0
LAG_EXP, LAG_SUM, LAG_DIVIDE = 1, 1, 2
LAG_P = 3
LAG_V = 3
LAG_TURN, LAG_PT = 5, 5
LAG_MIX, LAG_ADD = 6, 5
LAG_Q, LAG_QLOW, LAG_K, LAG_KLOW = -2, -1, -3, -2
FIRST = -3
MOST = 6
AHEAD = 10
CH = 448
NCH = PIX // CH
XT_BUFFERS = 4
W_TOP = 4.0
GN_EPS = 1e-5
SCALE = DH ** -0.5


def view(a, offset, dims):
    return bass.AP(a.tensor, a.offset + offset, [list(a.ap[0]), *[list(d) for d in dims]])


def window_attention(nc, x, qk_wt, v_wt, sel, grp, out):
    images = x.shape[0]
    x_d = x.rearrange("b (t p) h w -> b t p (h w)", p=P)
    out_d = out.rearrange("b (t p) h w -> b t p (h w)", p=P)

    ctx = ExitStack()
    with ctx:
        def sb(name, shape, dt):
            return ctx.enter_context(nc.sbuf_tensor(name, shape, dt))

        def pb(name, shape, dt=F32):
            return ctx.enter_context(nc.psum_tensor(name, shape, dt))

        def sem(name):
            return ctx.enter_context(nc.semaphore(name))

        img = sb("img", [P, 2, TILES, PIX], F32)
        xn_hi = sb("xn_hi", [P, 2, TILES, NW * NW * SLOT], F16)
        xn_lo = sb("xn_lo", [P, 2, TILES, NW * NW * SLOT], F16)
        q_hi = sb("q_hi", [P, 2, NW, P], F16)
        q_lo = sb("q_lo", [P, 2, NW, P], F16)
        k_hi = sb("k_hi", [P, 2, PIX], F16)
        k_lo = sb("k_lo", [P, 2, PIX], F16)
        k_f = sb("k_f", [P, 2, GROUP], F32)
        q_f = sb("q_f", [P, 2, GROUP], F32)
        w_f = sb("w_f", [P, TILES, 768], F32)
        w_hi = sb("w_hi", [P, TILES, 768], F16)
        w_lo = sb("w_lo", [P, TILES, 768], F16)
        select = sb("select", [P, TOK], F16)
        group_mean = sb("group_mean", [P, P], F32)
        smax = sb("smax", [P, 2, NW], F32)
        shifted = sb("shifted", [P, 2, GROUP], F32)
        exps = sb("exps", [P, 2, GROUP], F32)
        sums = sb("sums", [P, 2, NW], F32)
        rsum = sb("rsum", [P, 2, NW], F32)
        probs = sb("probs", [P, 2, GROUP], F32)
        p_hi = sb("p_hi", [P, 2, NW, P], F16)
        p_lo = sb("p_lo", [P, 2, NW, P], F16)
        pt = sb("pt", [P, 2, 2, GROUP], F16)
        v_hi = sb("v_hi", [P, 2, NW, P], F16)
        v_lo = sb("v_lo", [P, 2, NW, P], F16)
        bn = sb("bn", [P, TILES, NCH, 6], F32)
        mv = sb("mv", [P, 2, TILES], F32)
        dev = sb("dev", [P, 3, TILES], F32)
        gstat = sb("gstat", [P, 2, TILES], F32)
        norm = sb("norm", [P, 2, TILES], F32)
        xt = sb("xt", [P, XT_BUFFERS, GROUP], F32)
        ext = sb("ext", [P, 8], F32)
        ext_all = sb("ext_all", [P, 8], F32)
        amax = sb("amax", [P, 2], F32)
        inv_w = sb("inv_w", [P, 2], F32)
        mul_w = sb("mul_w", [P, 2], F32)
        sq_w = sb("sq_w", [P, 1], F32)
        exp_scale = sb("exp_scale", [P, 1], F32)
        v_scale = inv_w[:, 1:2]
        half = sb("half", [P, TILES], F32)

        ps_s = pb("ps_s", [P, 512])
        ps_q = pb("ps_q", [P, 512])
        ps_k = pb("ps_k", [P, 512])
        ps_v = [pb(f"ps_v{i}", [P, 512]) for i in range(2)]
        ps_t = pb("ps_t", [P, 2, 512])
        ps_o = pb("ps_o", [P, 512])
        ps_g = ps_k[:, 448:452]

        s_scores, s_max, s_shift, s_exp, s_sum, s_rsum, s_norm = map(
            sem, ("s_scores", "s_max", "s_shift", "s_exp", "s_sum", "s_rsum", "s_norm"))
        s_phi, s_plo_a, s_plo_b, s_turn, s_pt, s_v, s_vhi, s_vlo, s_mix, s_add = map(
            sem, ("s_phi", "s_plo_a", "s_plo_b", "s_turn", "s_pt", "s_v", "s_vhi", "s_vlo", "s_mix", "s_add"))
        s_q, s_k, s_qhi, s_qlo, s_khi, s_klo = map(sem, ("s_q", "s_k", "s_qhi", "s_qlo", "s_khi", "s_klo"))
        s_qlo_a = sem("s_qlo_a")
        s_bn, s_mv, s_mean, s_dev1, s_dev2, s_dev, s_var, s_gstat, s_rstd, s_nmean = map(
            sem, ("s_bn", "s_mv", "s_mean", "s_dev1", "s_dev2", "s_dev", "s_var", "s_gstat", "s_rstd", "s_nmean"))
        s_xt, s_xhi, s_xlo = map(sem, ("s_xt", "s_xhi", "s_xlo"))
        s_load = [sem(f"s_load{t}") for t in range(TILES)]
        s_store = [sem(f"s_store{t}") for t in range(TILES)]
        s_const, s_zero, s_half, s_ext, s_all, s_w, s_wprep = map(
            sem, ("s_const", "s_zero", "s_half", "s_ext", "s_all", "s_w", "s_wprep"))

        block = ctx.enter_context(nc.Block())

        class At:

            def __init__(self, it):
                self.it = it

            def step(self, g):
                return self.it * (2 * STEPS) + (AHEAD + g + 1)

            def keys(self, g):
                return self.it * 32 + (16 * (g // STEPS) + g % STEPS + 1)

            def pool_q(self, g):
                return self.it * (2 * len(POOL_Q)) + (len(POOL_Q) * (g // STEPS) + POOL_Q.index(g % STEPS) + 1)

            def image(self, m, per=1):
                return self.it * (2 * per) + (m + 1) * per

            def chunk(self, m, n):
                return self.it * 64 + (32 * m + n + 1)

        def place(g):
            s = g % STEPS
            return (g // STEPS) % 2, s // 16, (s // 2) % 8, s % 2

        def due(j, span):
            return span is None or span[0] <= j < span[1]

        def windows(a, dilated, r):
            if dilated:
                return view(a, SIDE * r, [[1, NW], [NW * SIDE, WS], [NW, WS]])
            return view(a, WS * SIDE * r, [[WS, NW], [SIDE, WS], [1, WS]])

        def tokens(a, dilated, r, w):
            if dilated:
                return view(a, SIDE * r + w, [[NW * SIDE, WS], [NW, WS]])
            return view(a, WS * SIDE * r + WS * w, [[SIDE, WS], [1, WS]])

        def in_rows(bank, dilated, w):
            if dilated:
                return view(bank[:, :], w, [[SIDE, WS], [NW, WS]])
            return view(bank[:, :], WS * w, [[SIDE, WS], [1, WS]])

        def rows(a, dilated, r):
            if dilated:
                return view(a, SIDE * r, [[NW * SIDE, WS], [1, SIDE]])
            return view(a, WS * SIDE * r, [[SIDE, WS], [1, SIDE]])

        def slotted(a, first=0, pitch=SLOT):
            return view(a, first, [[pitch, NW], [1, TOK]])

        def unwritten(a):
            n = NW * NW * SLOT
            return [bass.AP(a, TOK, [[4 * n, P], [SLOT, 4 * NW * NW], [1, SLOT - TOK]]),
                    bass.AP(a, 3 * n - 2 * NW * SLOT, [[4 * n, P], [n, TILES], [SLOT, 2 * NW], [1, TOK]])]

        def by_window(a):
            return a.rearrange("p (w t) -> p w t", t=TOK)

        def by_row(a):
            return a.rearrange("p (w a b) -> p w a b", w=NW, b=WS)

        STATS, n = {}, 0
        for at_step, count in zip(range(9, 17), (1, 1, 1, 2, 2, 2, 2, 3)):
            STATS[at_step] = [divmod(n + i, NCH) for i in range(count)]
            n += count
        assert n == TILES * NCH
        AGGREGATE, MEAN, DEVIATION, VARIANCE, SCALES = 17, 18, 18, 19, 19
        FIRST_CHUNK, FIRST_K, LAST_CHUNK = 20, STEPS + LAG_K, 37
        DOUBLE = 2 * (FIRST_K - FIRST_CHUNK)
        ORDER = [(FIRST_CHUNK + n // 2 if n < DOUBLE else
                  FIRST_K + (n - DOUBLE) * (LAST_CHUNK + 1 - FIRST_K) // (32 - DOUBLE),
                  n // 16, n % 16 // 2, n % 2) for n in range(32)]
        assert all(step - LAG_V >= 16 * kind + 2 * r + 1 for step, kind, r, t in ORDER)
        assert ORDER[31][0] <= STEPS + LAG_ADD
        BEFORE = sum(step < STEPS for step, *_ in ORDER)
        EARLY = 4

        POOL_Q = range(STEPS // 2 - 1, FIRST_CHUNK + 1)
        POOL_QB = range(STEPS // 2 - 1, AGGREGATE + 2)

        def q_by_pool(j):
            return j % STEPS in POOL_Q

        def q_by_pool_only(j):
            return j % STEPS in POOL_QB

        def chunk_of(dil, r):
            return 16 * dil + 2 * r + 1

        def chunks(g, span):
            s = g % STEPS
            return [(g // STEPS + (step < STEPS), n, kind, r, t) for n, (step, kind, r, t) in enumerate(ORDER)
                    if step % STEPS == s and due(g, span)]

        @block.sync
        def _(sp):
            def load(i, t, par):
                sp.dma_start(img[:, par, t, :], x_d[i, t]).then_inc(s_load[t], 16)

            def store(i, t, par):
                sp.dma_start(out_d[i, t], img[:, par, t, :]).then_inc(s_store[t], 16)

            for t in range(TILES):
                load(0, t, 0)
            for t in range(TILES):
                sp.wait_ge(s_load[t], 16)
                load(1, t, 1)

            def image(at, m, nxt):
                for t in range(TILES):
                    sp.wait_ge(s_add, at.step(m * STEPS + STEPS - TILES + t))
                    store(at.it * 2 + m, t, m)
                if nxt is not None:
                    for t in range(TILES):
                        sp.wait_ge(s_store[t], at.it * 32 + 16 * (m + 1))
                        load(nxt, t, m)

            with sp.Fori(0, images // 2 - 1) as it:
                for m in range(2):
                    image(At(it), m, it * 2 + (m + 2))
            image(At(images // 2 - 1), 0, images - 1)
            image(At(images // 2 - 1), 1, None)
            for t in range(TILES):
                sp.wait_ge(s_store[t], 16 * images)

        @block.tensor
        def _(pe):
            mm = nc.tensor.matmul

            def three(o, stat, mov, first, last):
                mm(o, stat[0], mov[0], start=first, stop=False)
                mm(o, stat[0], mov[1], start=False, stop=False)
                return mm(o, stat[1], mov[0], start=False, stop=last)

            def project(bank, dil, r, hp, col):
                for c in range(TILES):
                    w = slice(col + P * hp, col + P * hp + P)
                    mov = [slotted(a[:, dil, c, :], r * NW * SLOT) for a in (xn_hi, xn_lo)]
                    last = three(bank[:, 0:GROUP], (w_hi[:, c, w], w_lo[:, c, w]), mov, c == 0, c == TILES - 1)
                return last

            def project_q(at, g):
                m, dil, r, hp = place(g)
                if dil:
                    pe.wait_ge(s_xlo, at.chunk(g // STEPS, chunk_of(dil, r)))
                pe.wait_ge(s_qhi if q_by_pool_only(g - 1) else s_qlo, at.step(g - 1))
                project(ps_q, dil, r, hp, 0).then_inc(s_q, 1)

            def project_k(at, g, wait=True):
                m, dil, r, hp = place(g)
                if hp == 0:
                    pe.wait_ge(s_xlo, at.chunk(g // STEPS, chunk_of(dil, r)))
                if wait:
                    pe.wait_ge(s_khi, at.keys(g) - 1)
                project(ps_k, dil, r, hp, 256).then_inc(s_k, 1)

            def mean(at, m):
                pe.wait_ge(s_mv, at.image(m))
                mm(ps_g[:, 0:2], group_mean[:], mv[:, 0, :], start=True, stop=True).then_inc(s_mean, 1)

            def variance(at, m):
                pe.wait_ge(s_dev, at.image(m))
                mm(ps_g[:, 2:4], group_mean[:], dev[:, 2, :], start=True, stop=True).then_inc(s_var, 1)

            def scores(at, g):
                m, dil, r, hp = place(g)
                pe.wait_ge(s_qlo, at.step(g))
                if q_by_pool(g):
                    pe.wait_ge(s_qlo_a, at.pool_q(g))
                if not dil:
                    pe.wait_ge(s_klo, at.keys(g))
                pe.wait_ge(s_shift, at.step(g - 1))
                for w in range(NW):
                    f = three(ps_s[:, w * TOK:w * TOK + TOK], (q_hi[:, g % 2, w, :], q_lo[:, g % 2, w, :]),
                              [tokens(a[:, hp, :], dil, r, w) for a in (k_hi, k_lo)], True, True)
                f.then_inc(s_scores, 1)

            def turn(at, g):
                pe.wait_ge(s_plo_b, at.step(g))
                pe.wait_ge(s_pt, at.step(g - 1))
                for k, part in enumerate((p_hi, p_lo)):
                    for w in range(NW):
                        f = mm(ps_t[:, k, w * TOK:w * TOK + TOK], part[:, g % 2, w, :], select[:],
                               start=True, stop=True)
                f.then_inc(s_turn, 1)

            def values(at, g):
                m, dil, r, hp = place(g)
                pe.wait_ge(s_vlo, at.step(g - 2))
                cols = slice(512 + P * hp, 512 + P * hp + P)
                for w in range(0, NW, 2):
                    for c in range(TILES):
                        at_w = slice((r * NW + w) * SLOT, (r * NW + w + 2) * SLOT)
                        f = three(ps_v[g % 2][:, w * DH:w * DH + P], [a[:, dil, c, at_w] for a in (xn_hi, xn_lo)],
                                  (w_hi[:, c, cols], w_lo[:, c, cols]), c == 0, c == TILES - 1)
                f.then_inc(s_v, 1)

            def mix(at, g):
                m, dil, r, hp = place(g)
                pe.wait_ge(s_add, at.step(g - 1))
                pe.wait_ge(s_pt, at.step(g))
                pe.wait_ge(s_vlo, at.step(g))
                for w in range(NW):
                    t = slice(w * TOK, w * TOK + TOK)
                    f = three(in_rows(ps_o, dil, w), (v_hi[:, g % 2, w, :], v_lo[:, g % 2, w, :]),
                              (pt[:, g % 2, 0, t], pt[:, g % 2, 1, t]), True, True)
                f.then_inc(s_mix, 1)

            def step(at, g, span=None):
                if due(g - LAG_MIX, span):
                    mix(at, g - LAG_MIX)
                if due(g - LAG_TURN, span):
                    turn(at, g - LAG_TURN)
                if g % STEPS == VARIANCE and due(g, span):
                    variance(at, g // STEPS + 1)
                if due(g - LAG_V, span):
                    values(at, g - LAG_V)
                if due(g - LAG_SCORES, span):
                    scores(at, g - LAG_SCORES)
                if g % STEPS == MEAN and due(g, span):
                    mean(at, g // STEPS + 1)
                if due(g - LAG_Q, span):
                    project_q(at, g - LAG_Q)
                if due(g - LAG_K, span) and not place(g - LAG_K)[1]:
                    project_k(at, g - LAG_K, g > LAG_K)

            zero = At(0)
            pe.wait_ge(s_const, 32)
            mean(zero, 0)
            variance(zero, 0)
            pe.wait_ge(s_wprep, 3)
            pe.wait_ge(s_zero, ZEROS)
            for g in range(FIRST, 0):
                step(zero, g, (0, STEPS))
            with pe.Fori(0, images // 2) as it:
                for g in range(2 * STEPS):
                    step(At(it), g)
            for g in range(2 * STEPS, 2 * STEPS + MOST):
                step(At(images // 2 - 1), g, (0, 2 * STEPS))

        @block.scalar
        def _(act):
            def copy(o, i):
                return nc.scalar.activation(o, i, ACT.Copy)

            def q_part(at, g):
                act.wait_ge(s_q, at.step(g))
                if q_by_pool(g):
                    o = slice(0, P if q_by_pool_only(g) else 64)
                    copy(q_f[o, g % 2, :], ps_q[o, 0:GROUP])
                for h in range(2):
                    o = slice(64 * h, 64 * h + 64)
                    f = copy(slotted(q_hi[o, g % 2, 0, :], 64 * h, P), by_window(ps_q[o, 0:GROUP]))
                f.then_inc(s_qhi, 1)

            def k_part(at, g, wait):
                m, dil, r, hp = place(g)
                act.wait_ge(s_k, at.keys(g))
                copy(windows(k_hi[:, hp, :], dil, r), by_row(ps_k[:, 0:GROUP]))
                if wait:
                    act.wait_ge(s_klo, at.keys(g) - 2)
                copy(k_f[:, g % 2, :], ps_k[:, 0:GROUP]).then_inc(s_khi, 1)

            def x_part(at, m, n, kind, r, t):
                act.wait_ge(s_xt, at.chunk(m, n))
                copy(slotted(xn_hi[:, kind, t, :], r * NW * SLOT), by_window(xt[:, n % XT_BUFFERS, :])).then_inc(s_xhi, 1)

            def p_part(at, g):
                act.wait_ge(s_norm, at.step(g))
                for h in range(2):
                    o = slice(64 * h, 64 * h + 64)
                    f = copy(slotted(p_hi[o, g % 2, 0, :], 64 * h, P), by_window(probs[o, g % 2, :]))
                f.then_inc(s_phi, 1)

            def turned(at, g):
                act.wait_ge(s_turn, at.step(g))
                copy(pt[:, g % 2, :, :], ps_t[:, :, 0:GROUP]).then_inc(s_pt, 1)

            def exp(at, g):
                act.wait_ge(s_shift, at.step(g))
                nc.scalar.activation(exps[:, g % 2, :], shifted[:, g % 2, :], ACT.Exp,
                                     scale=exp_scale[:, 0:1]).then_inc(s_exp, 1)

            def v_part(at, g):
                act.wait_ge(s_v, at.step(g))
                act.wait_ge(s_mix, at.step(g - 2))
                for odd in range(2):
                    for h in range(2):
                        src = ps_v[g % 2][64 * odd:64 * odd + 64, :].rearrange("p (j n) -> p j n", n=P)
                        f = nc.scalar.activation(v_hi[64 * h:64 * h + 64, g % 2, odd::2, DH * h:DH * h + DH],
                                                 src[:, :, DH * h:DH * h + DH], ACT.Relu)
                f.then_inc(s_vhi, 1)

            def step(at, g, span=None):
                if due(g - LAG_PT, span):
                    turned(at, g - LAG_PT)
                if due(g - LAG_P, span):
                    p_part(at, g - LAG_P)
                if due(g - LAG_EXP, span):
                    exp(at, g - LAG_EXP)
                if due(g - LAG_Q, span):
                    q_part(at, g - LAG_Q)
                if due(g - LAG_K, span) and not place(g - LAG_K)[1]:
                    k_part(at, g - LAG_K, g >= 0 or g > LAG_K + 1)
                if due(g - LAG_V, span):
                    v_part(at, g - LAG_V)
                for chunk in chunks(g, span):
                    x_part(at, *chunk)

            act.dma_start(w_f[:, :, 0:512], qk_wt.rearrange("(t p) n -> p t n", p=P)).then_inc(s_w, 16)
            act.dma_start(w_f[:, :, 512:768], v_wt.rearrange("(t p) n -> p t n", p=P)).then_inc(s_w, 16)
            act.dma_start(select[:], sel).then_inc(s_const, 16)
            act.dma_start(group_mean[:], grp).then_inc(s_const, 16)
            zero = At(0)
            act.wait_ge(s_zero, ZEROS)
            def part(some):
                for n in some:
                    x_part(zero, 0, n, *ORDER[n][1:])

            part(range(EARLY))
            for g in range(FIRST, 0):
                step(zero, g, (0, STEPS))
            part(range(EARLY, BEFORE))
            act.wait_ge(s_wprep, 3)
            with act.Fori(0, images // 2) as it:
                for g in range(2 * STEPS):
                    step(At(it), g)
            for g in range(2 * STEPS, 2 * STEPS + MOST):
                step(At(images // 2 - 1), g, (0, 2 * STEPS))

        @block.vector
        def _(dve):
            V = nc.vector

            def q_part(at, g):
                if g % STEPS == POOL_QB[-1] + 1:
                    dve.wait_ge(s_qlo, at.step(g - 1))
                dve.wait_ge(s_qhi, at.step(g))
                for h in range(1 if q_by_pool(g) else 0, 2):
                    o = slice(64 * h, 64 * h + 64)
                    f = V.tensor_tensor(slotted(q_lo[o, g % 2, 0, :], 64 * h, P), by_window(ps_q[o, 0:GROUP]),
                                        slotted(q_hi[o, g % 2, 0, :], 64 * h, P), ALU.subtract)
                f.then_inc(s_qlo, 1)

            def stats(at, m, t, c):
                if c == 0:
                    dve.wait_ge(s_load[t], at.image(m, 16))
                V.bn_stats(bn[:, t, c, :], img[:, m % 2, t, c * CH:c * CH + CH]).then_inc(s_bn, 1)

            def aggregate(at, m):
                for t in range(TILES):
                    f = V.bn_aggr(mv[:, :, t], bn[:, t, :, :])
                f.then_inc(s_mv, 1)

            def deviation(at, m):
                dve.wait_ge(s_mean, at.image(m))
                V.tensor_tensor(dev[:, 0, :], ps_g[:, 0:2], mv[:, 0, :], ALU.subtract)
                V.tensor_scalar(gstat[:, 0, :], ps_g[:, 0:2], -1.0, None, ALU.mult).then_inc(s_dev1, 1)
                dve.wait_ge(s_dev1, at.image(m))
                V.tensor_tensor(dev[:, 1, :], dev[:, 0, :], dev[:, 0, :], ALU.mult).then_inc(s_dev2, 1)
                dve.wait_ge(s_dev2, at.image(m))
                V.tensor_tensor(dev[:, 2, :], dev[:, 1, :], mv[:, 1, :], ALU.add).then_inc(s_dev, 1)

            def group_variance(at, m):
                dve.wait_ge(s_var, at.image(m))
                V.tensor_scalar(gstat[:, 1, :], ps_g[:, 2:4], GN_EPS, None, ALU.add).then_inc(s_gstat, 1)

            def largest(at, g):
                dve.wait_ge(s_scores, at.step(g))
                V.tensor_reduce(smax[:, g % 2, :], by_window(ps_s[:, 0:GROUP]), axis=AX, op=ALU.max).then_inc(s_max, 1)

            def shift(at, g):
                dve.wait_ge(s_max, at.step(g))
                V.tensor_tensor(by_window(shifted[:, g % 2, :]), by_window(ps_s[:, 0:GROUP]),
                                smax[:, g % 2, :].unsqueeze(2).to_broadcast([P, NW, TOK]),
                                ALU.subtract).then_inc(s_shift, 1)

            def total(at, g):
                dve.wait_ge(s_exp, at.step(g))
                V.tensor_reduce(sums[:, g % 2, :], by_window(exps[:, g % 2, :]), axis=AX, op=ALU.add).then_inc(s_sum, 1)

            def inverse(at, g):
                dve.wait_ge(s_sum, at.step(g))
                V.reciprocal(rsum[:, g % 2, :], sums[:, g % 2, :]).then_inc(s_rsum, 1)

            def normed(at, m, n, kind, r, t, first=False):
                if n == 0:
                    dve.wait_ge(s_nmean, at.image(m))
                if not first:
                    dve.wait_ge(s_xlo, at.chunk(m, n - XT_BUFFERS))
                V.tensor_scalar(by_row(xt[:, n % XT_BUFFERS, :]), windows(img[:, m % 2, t, :], kind, r), norm[:, 0, t:t + 1],
                                norm[:, 1, t:t + 1], ALU.mult, ALU.add).then_inc(s_xt, 1)

            def v_part(at, g):
                dve.wait_ge(s_vhi, at.step(g))
                for odd in range(2):
                    for h in range(2):
                        src = ps_v[g % 2][64 * odd:64 * odd + 64, :].rearrange("p (j n) -> p j n", n=P)
                        at_h = (slice(64 * h, 64 * h + 64), g % 2, slice(odd, NW, 2), slice(DH * h, DH * h + DH))
                        f = V.scalar_tensor_tensor(v_lo[at_h], src[:, :, DH * h:DH * h + DH], 0.0, v_hi[at_h],
                                                   ALU.max, ALU.subtract)
                f.then_inc(s_vlo, 1)

            def add(at, g):
                m, dil, r, hp = place(g)
                acc = rows(img[:, m, hp, :], dil, r)
                dve.wait_ge(s_mix, at.step(g))
                V.scalar_tensor_tensor(acc, ps_o[:, 0:GROUP].rearrange("p (a b) -> p a b", b=SIDE), v_scale, acc,
                                       ALU.mult, ALU.add).then_inc(s_add, 1)

            def step(at, g, span=None):
                if g % STEPS == AGGREGATE and due(g, span):
                    dve.wait_ge(s_bn, at.image(g // STEPS + 1, TILES * NCH))
                if g % STEPS == DEVIATION and due(g, span):
                    deviation(at, g // STEPS + 1)
                if due(g - LAG_MAX, span):
                    largest(at, g - LAG_MAX)
                if due(g - LAG_SUM, span):
                    total(at, g - LAG_SUM)
                if due(g - LAG_SHIFT, span):
                    shift(at, g - LAG_SHIFT)
                if g % STEPS == SCALES and due(g, span):
                    group_variance(at, g // STEPS + 1)
                if due(g, span):
                    if g % STEPS == AGGREGATE:
                        aggregate(at, g // STEPS + 1)
                    for t, c in STATS.get(g % STEPS, ()):
                        stats(at, g // STEPS + 1, t, c)
                for chunk in chunks(g, span):
                    normed(at, *chunk)
                if due(g - LAG_Q, span) and not q_by_pool_only(g - LAG_Q):
                    q_part(at, g - LAG_Q)
                if due(g - LAG_SUM, span):
                    inverse(at, g - LAG_SUM)
                if due(g - LAG_ADD, span):
                    add(at, g - LAG_ADD)
                if due(g - LAG_V, span):
                    v_part(at, g - LAG_V)

            def zeros(a):
                V.memset(a, 0.0).then_inc(s_zero, 1)

            for a in unwritten(xn_hi):
                zeros(a)
            zeros(q_hi[:, :, :].bitcast(F32))
            zeros(p_hi[:, :, :, :].bitcast(F32))
            zeros(pt[:, :, :, :].bitcast(F32))
            zeros(shifted[:, :, :])
            zeros(rsum[:, :, :])
            zero = At(0)
            for t in range(TILES):
                for c in range(NCH):
                    stats(zero, 0, t, c)
            dve.wait_ge(s_bn, TILES * NCH)
            aggregate(zero, 0)
            deviation(zero, 0)
            group_variance(zero, 0)
            dve.wait_ge(s_w, 32)
            for n, (cols, op) in enumerate((((0, 512), ALU.max), ((0, 512), ALU.min), ((512, 768), ALU.max), ((512, 768), ALU.min))):
                V.tensor_reduce(ext[:, 2 * n:2 * n + 2], w_f[:, :, cols[0]:cols[1]], axis=AX, op=op).then_inc(s_ext, 1)
            dve.wait_ge(s_all, 1)
            V.tensor_reduce(amax[:], ext_all[:].rearrange("p (a b) -> p a b", b=4), axis=AX, op=ALU.max).then_inc(s_ext, 1)
            dve.wait_ge(s_ext, 5)
            V.tensor_scalar(inv_w[:], amax[:], 1e-30, 1.0 / W_TOP, ALU.max, ALU.mult).then_inc(s_ext, 1)
            dve.wait_ge(s_ext, 6)
            V.reciprocal(mul_w[:], inv_w[:]).then_inc(s_ext, 1)
            V.tensor_tensor(sq_w[:], inv_w[:, 0:1], inv_w[:, 0:1], ALU.mult).then_inc(s_ext, 1)
            dve.wait_ge(s_ext, 8)
            V.tensor_scalar(exp_scale[:], sq_w[:], SCALE, None, ALU.mult).then_inc(s_wprep, 1)
            for n, cols in enumerate(((0, 512), (512, 768))):
                V.tensor_scalar(w_f[:, :, cols[0]:cols[1]], w_f[:, :, cols[0]:cols[1]], mul_w[:, n:n + 1], None,
                                ALU.mult).then_inc(s_ext, 1)
            dve.wait_ge(s_ext, 10)
            V.tensor_copy(w_hi[:], w_f[:]).then_inc(s_wprep, 1)
            dve.wait_ge(s_wprep, 2)
            V.tensor_tensor(w_lo[:], w_f[:], w_hi[:], ALU.subtract).then_inc(s_wprep, 1)
            dve.wait_ge(s_zero, ZEROS)
            def part(some):
                for n in some:
                    normed(zero, 0, n, *ORDER[n][1:], n < XT_BUFFERS)

            part(range(EARLY))
            for g in range(FIRST, 0):
                step(zero, g, (0, STEPS))
            part(range(EARLY, BEFORE))
            for t in range(TILES):
                dve.wait_ge(s_load[t], 32)
            with dve.Fori(0, images // 2) as it:
                for g in range(2 * STEPS):
                    step(At(it), g)
            for g in range(2 * STEPS, 2 * STEPS + MOST):
                step(At(images // 2 - 1), g, (0, 2 * STEPS))

        @block.gpsimd
        def _(pool):
            G = nc.gpsimd

            def scale_of(at, m):
                pool.wait_ge(s_gstat, at.image(m))
                G.tensor_tensor(out=norm[:, 0, :], in0=gstat[:, 1, :], in1=half[:], op=ALU.pow).then_inc(s_rstd, 1)
                pool.wait_ge(s_rstd, at.image(m))
                G.tensor_tensor(out=norm[:, 1, :], in0=gstat[:, 0, :], in1=norm[:, 0, :],
                                op=ALU.mult).then_inc(s_nmean, 1)

            def low(at, m, n, kind, r, t):
                pool.wait_ge(s_xhi, at.chunk(m, n))
                G.tensor_tensor(out=slotted(xn_lo[:, kind, t, :], r * NW * SLOT), in0=by_window(xt[:, n % XT_BUFFERS, :]),
                                in1=slotted(xn_hi[:, kind, t, :], r * NW * SLOT), op=ALU.subtract).then_inc(s_xlo, 1)

            def divide(at, g):
                pool.wait_ge(s_rsum, at.step(g))
                pool.wait_ge(s_plo_a, at.step(g - 2))
                pool.wait_ge(s_plo_b, at.step(g - 1 + LAG_DIVIDE - LAG_P))
                G.tensor_tensor(out=by_window(probs[:, g % 2, :]), in0=by_window(exps[:, g % 2, :]),
                                in1=rsum[:, g % 2, :].unsqueeze(2).to_broadcast([P, NW, TOK]),
                                op=ALU.mult).then_inc(s_norm, 1)

            def p_part(at, g):
                o = slice(0, 64)
                pool.wait_ge(s_phi, at.step(g))
                G.tensor_tensor(out=slotted(p_lo[o, g % 2, 0, :], 0, P), in0=by_window(probs[o, g % 2, :]),
                                in1=slotted(p_hi[o, g % 2, 0, :], 0, P), op=ALU.subtract).then_inc(s_plo_a, 1)

            def q_part(at, g):
                pool.wait_ge(s_qhi, at.step(g))
                G.tensor_tensor(out=slotted(q_lo[0:64, g % 2, 0, :], 0, P), in0=by_window(q_f[0:64, g % 2, :]),
                                in1=slotted(q_hi[0:64, g % 2, 0, :], 0, P), op=ALU.subtract).then_inc(s_qlo_a, 1)

            def q_part_b(at, g):
                o = slice(64, P)
                if g % STEPS == POOL_QB[0]:
                    pool.wait_ge(s_qlo, at.step(g - 1))
                pool.wait_ge(s_qlo_a, at.pool_q(g))
                G.tensor_tensor(out=slotted(q_lo[o, g % 2, 0, :], 64, P), in0=by_window(q_f[o, g % 2, :]),
                                in1=slotted(q_hi[o, g % 2, 0, :], 64, P), op=ALU.subtract).then_inc(s_qlo, 1)

            def k_part(at, g):
                m, dil, r, hp = place(g)
                pool.wait_ge(s_khi, at.keys(g))
                G.tensor_tensor(out=windows(k_lo[:, hp, :], dil, r), in0=by_row(k_f[:, g % 2, :]),
                                in1=windows(k_hi[:, hp, :], dil, r), op=ALU.subtract).then_inc(s_klo, 1)

            def p_part_b(at, g):
                o = slice(64, P)
                pool.wait_ge(s_plo_a, at.step(g))
                G.tensor_tensor(out=slotted(p_lo[o, g % 2, 0, :], 64, P), in0=by_window(probs[o, g % 2, :]),
                                in1=slotted(p_hi[o, g % 2, 0, :], 64, P), op=ALU.subtract).then_inc(s_plo_b, 1)

            def step(at, g, span=None):
                if due(g - LAG_DIVIDE, span):
                    divide(at, g - LAG_DIVIDE)
                if due(g - LAG_QLOW, span) and q_by_pool(g - LAG_QLOW):
                    q_part(at, g - LAG_QLOW)
                if due(g - LAG_QLOW, span) and q_by_pool_only(g - LAG_QLOW):
                    q_part_b(at, g - LAG_QLOW)
                    pool.wait_ge(s_qlo, at.step(g - LAG_QLOW))
                if due(g - LAG_KLOW, span) and not place(g - LAG_KLOW)[1]:
                    k_part(at, g - LAG_KLOW)
                if due(g - LAG_P, span):
                    p_part(at, g - LAG_P)
                if due(g - LAG_P, span):
                    p_part_b(at, g - LAG_P)
                    if chunks(g, span) or g % STEPS == SCALES or not due(g + 1 - LAG_DIVIDE, span):
                        pool.wait_ge(s_plo_b, at.step(g - LAG_P))
                for chunk in chunks(g, span):
                    low(at, *chunk)
                if g % STEPS == SCALES and due(g, span):
                    scale_of(at, g // STEPS + 1)
            G.memset(half[:], -0.5).then_inc(s_half, 1)
            for a in unwritten(xn_lo):
                G.memset(a, 0.0).then_inc(s_zero, 1)
            G.memset(q_lo[:, :, :].bitcast(F32), 0.0).then_inc(s_zero, 1)
            G.memset(p_lo[:, :, :, :].bitcast(F32), 0.0).then_inc(s_zero, 1)
            G.memset(v_hi[:, :, :, :].bitcast(F32), 0.0).then_inc(s_zero, 1)
            G.memset(v_lo[:, :, :, :].bitcast(F32), 0.0).then_inc(s_zero, 1)
            G.memset(probs[:, :, :], 0.0).then_inc(s_zero, 1)
            G.memset(exps[:, :, :], 1.0).then_inc(s_zero, 1)
            for lag, stages in ((LAG_SCORES, (s_q, s_qhi, s_qlo, s_scores, s_max, s_shift)),
                                (LAG_EXP, (s_exp, s_sum, s_rsum)), (LAG_DIVIDE, (s_norm,)),
                                (LAG_P, (s_phi, s_plo_a, s_plo_b)), (LAG_V, (s_v, s_vhi, s_vlo)), (LAG_TURN, (s_turn, s_pt)),
                                (LAG_MIX, (s_mix,)), (LAG_ADD, (s_add,))):
                for s in stages:
                    pool.sem_inc(s, AHEAD - lag)
            pool.wait_ge(s_half, 1)
            pool.wait_ge(s_ext, 4)
            G.partition_all_reduce(ext_all[:], ext[:], P, bass.bass_isa.ReduceOp.absmax).then_inc(s_all, 1)
            zero = At(0)
            scale_of(zero, 0)
            for n in range(EARLY):
                low(zero, 0, n, *ORDER[n][1:])
            for g in range(FIRST, 0):
                step(zero, g, (0, STEPS))
            for n in range(EARLY, BEFORE):
                low(zero, 0, n, *ORDER[n][1:])
            with pool.Fori(0, images // 2) as it:
                for g in range(2 * STEPS):
                    step(At(it), g)
            for g in range(2 * STEPS, 2 * STEPS + MOST):
                step(At(images // 2 - 1), g, (0, 2 * STEPS))


def kernel(x, L0_conv_qk_w, L0_conv_v_w):
    import numpy as np
    import concourse.bacc as bacc
    from concourse.bass_utils import run_bass_kernel_spmd

    sel = np.zeros((P, TOK), np.float16)
    for h in range(2):
        for a in range(WS):
            for b in range(WS):
                sel[SLOT * h + WS * a + b, WS * a + b] = 1
    grp = np.kron(np.eye(P // 8), np.full((8, 8), 0.125)).astype(np.float32)
    nc = bacc.Bacc("TRN2", target_bir_lowering=False, num_devices=1)
    arrays = {
        "x_dram": np.ascontiguousarray(x),
        "qk_wt_dram": np.ascontiguousarray(np.asarray(L0_conv_qk_w).T),
        "v_wt_dram": np.ascontiguousarray(np.asarray(L0_conv_v_w).T),
        "sel_dram": sel,
        "grp_dram": grp,
    }
    args = [nc.dram_tensor(n, a.shape, mybir.dt.from_np(a.dtype), kind="ExternalInput").ap()
            for n, a in arrays.items()]
    out = nc.dram_tensor("out_dram", arrays["x_dram"].shape, F32, kind="ExternalOutput").ap()
    window_attention(nc, *args, out)
    r = run_bass_kernel_spmd(nc, [arrays], core_ids=[0])
    return r.results[0]["out_dram"]
```
